# Optimizing a Trainium2 kernel written in Bass

```python
import numpy as np
import jax
import jax.numpy as jnp

def _softmax(x, axis=-1):
    return jax.nn.softmax(x, axis=axis)

def _gelu(x):
    return jax.nn.gelu(x, approximate=True)

def _silu(x):
    return jax.nn.silu(x)

def _sigmoid(x):
    return jax.nn.sigmoid(x)

def _layernorm(x, axis=-1, eps=1e-05):
    m = jnp.mean(x, axis=axis, keepdims=True)
    v = jnp.var(x, axis=axis, keepdims=True)
    return (x - m) / jnp.sqrt(v + eps)

def _scatter_add(tgt, idx, src, axis=0):
    return tgt.at[idx].add(src)

def _segment_sum(src, seg, n):
    return jax.ops.segment_sum(src, seg, n)
kernel_name = 'mk_decoder_preln_d1_seqx_r8_0b6122'

def setup_inputs(seed: int=0):
    np.random.seed(seed)
    _w = jnp.asarray

    def _rec_inputs():
        import jax
        import jax.numpy as jnp
        _rk = jax.random.key(seed)
        x = 7.22e-05 + 1 * jax.random.normal(jax.random.fold_in(_rk, 1), (4, 256, 128), jnp.float32)
        _lenS = 256 - jax.random.randint(jax.random.fold_in(_rk, 7), (4,), 0, max(1, 256 // 4) + 1, jnp.int32)
        _lenS2 = 1601 - jax.random.randint(jax.random.fold_in(_rk, 8), (4,), 0, max(1, 1601 // 4) + 1, jnp.int32)
        _ctx_1024P = jax.random.normal(jax.random.fold_in(_rk, 11), (4, 16, 128), jnp.float32)
        _ctx_1024c = jax.random.dirichlet(jax.random.fold_in(_rk, 511), 0.3 * jnp.ones((16,), jnp.float32), (4, 1601))
        _ctx_1024t = jnp.einsum('bsk,bkd->bsd', _ctx_1024c, _ctx_1024P)
        _ctx_1024t = _ctx_1024t * jax.lax.rsqrt(jnp.mean(jnp.square(_ctx_1024t)) + 1e-12) * 0.953939
        ctx_1024 = 4.13588e-05 + 0.999923 * (_ctx_1024t + 0.3 * jax.random.normal(jax.random.fold_in(_rk, 611), (4, 1601, 128), jnp.float32))
        return (x, ctx_1024)
    x, ctx_1024 = _rec_inputs()

    def _L0_attn_setup():
        import jax, jax.numpy as jnp
        import numpy as np
        import math
        D_K = 64
        key = jax.random.key(seed)
        ks = jax.random.split(key, 5)
        b, m, d, h, dk, dv = (8, 128, 128, 16, 64, 64)
        return {'x': jax.random.normal(ks[0], (b, m, d), dtype=jnp.float32), 'P_q': jax.random.normal(ks[1], (h, d, dk), dtype=jnp.float32) * 0.02, 'P_k': jax.random.normal(ks[2], (h, d, dk), dtype=jnp.float32) * 0.02, 'P_v': jax.random.normal(ks[3], (h, d, dv), dtype=jnp.float32) * 0.02, 'P_o': jax.random.normal(ks[4], (h, d, dv), dtype=jnp.float32) * 0.02}
    _L0_attn_all = _L0_attn_setup()
    _L0_attn_in = {k: v for k, v in _L0_attn_all.items() if k in ('P_q', 'P_k', 'P_v', 'P_o')}
    del _L0_attn_all

    def _L0_xattn_setup():
        import jax, jax.numpy as jnp
        import numpy as np
        N_HEAD, MODEL_DIM, KEY_DIM, VALUE_DIM = (16, 128, 64, 64)
        B, S = (4, 256)
        EPS = 1e-05
        TEMP = float(np.sqrt(KEY_DIM))
        key = jax.random.key(seed)
        ks = jax.random.split(key, 12)
        d = {'query': jax.random.normal(ks[0], (B, S, MODEL_DIM), jnp.float32), 'key': jax.random.normal(ks[1], (B, S, MODEL_DIM), jnp.float32), 'value': jax.random.normal(ks[2], (B, S, MODEL_DIM), jnp.float32), 'Wq': jax.random.normal(ks[3], (MODEL_DIM, N_HEAD * KEY_DIM), jnp.float32) * np.sqrt(2.0 / (MODEL_DIM + KEY_DIM)), 'bq': jnp.zeros((N_HEAD * KEY_DIM,), jnp.float32), 'Wk': jax.random.normal(ks[4], (MODEL_DIM, N_HEAD * KEY_DIM), jnp.float32) * np.sqrt(2.0 / (MODEL_DIM + KEY_DIM)), 'bk': jnp.zeros((N_HEAD * KEY_DIM,), jnp.float32), 'Wv': jax.random.normal(ks[5], (MODEL_DIM, N_HEAD * VALUE_DIM), jnp.float32) * np.sqrt(2.0 / (MODEL_DIM + VALUE_DIM)), 'bv': jnp.zeros((N_HEAD * VALUE_DIM,), jnp.float32), 'Wo': jax.random.normal(ks[6], (N_HEAD * VALUE_DIM, MODEL_DIM), jnp.float32) * np.sqrt(2.0 / (N_HEAD * VALUE_DIM + MODEL_DIM)), 'bo': jnp.zeros((MODEL_DIM,), jnp.float32), 'ln_gamma': jnp.ones((MODEL_DIM,), jnp.float32), 'ln_beta': jnp.zeros((MODEL_DIM,), jnp.float32)}
        return d
    _L0_xattn_all = _L0_xattn_setup()
    _L0_xattn_in = {k: v for k, v in _L0_xattn_all.items() if k in ('Wq', 'bq', 'Wk', 'bk', 'Wv', 'bv', 'Wo', 'bo', 'ln_gamma', 'ln_beta')}
    del _L0_xattn_all

    def _L0_ffn_setup():
        import jax, jax.numpy as jnp
        import numpy as np
        DIM = 128
        HIDDEN = 384
        SCALE = 1.0 / 127.0

        def _dequant(w_int, dtype):
            return w_int.astype(dtype) * jnp.asarray(SCALE, dtype)
        key = jax.random.key(seed)
        k_x, k_g, k_u, k_d = jax.random.split(key, 4)
        x = jax.random.normal(k_x, (4, 256, DIM), dtype=jnp.float32)
        w_gate = jax.random.randint(k_g, (HIDDEN, DIM), -127, 128, dtype=jnp.int32)
        w_up = jax.random.randint(k_u, (HIDDEN, DIM), -127, 128, dtype=jnp.int32)
        w_down = jax.random.randint(k_d, (DIM, HIDDEN), -127, 128, dtype=jnp.int32)
        return {'x': x, 'w_gate': w_gate, 'w_up': w_up, 'w_down': w_down}
    _L0_ffn_all = _L0_ffn_setup()
    _L0_ffn_in = {k: v for k, v in _L0_ffn_all.items() if k in ('w_gate', 'w_up', 'w_down')}
    del _L0_ffn_all
    return {'x': x, 'ctx_1024': ctx_1024, 'L0_attn_P_q': _L0_attn_in['P_q'], 'L0_attn_P_k': _L0_attn_in['P_k'], 'L0_attn_P_v': _L0_attn_in['P_v'], 'L0_attn_P_o': _L0_attn_in['P_o'], 'L0_xattn_Wq': _L0_xattn_in['Wq'], 'L0_xattn_bq': _L0_xattn_in['bq'], 'L0_xattn_Wk': _L0_xattn_in['Wk'], 'L0_xattn_bk': _L0_xattn_in['bk'], 'L0_xattn_Wv': _L0_xattn_in['Wv'], 'L0_xattn_bv': _L0_xattn_in['bv'], 'L0_xattn_Wo': _L0_xattn_in['Wo'], 'L0_xattn_bo': _L0_xattn_in['bo'], 'L0_xattn_ln_gamma': _L0_xattn_in['ln_gamma'], 'L0_xattn_ln_beta': _L0_xattn_in['ln_beta'], 'L0_ffn_w_gate': _L0_ffn_in['w_gate'], 'L0_ffn_w_up': _L0_ffn_in['w_up'], 'L0_ffn_w_down': _L0_ffn_in['w_down']}

def reference(x, ctx_1024, L0_attn_P_q, L0_attn_P_k, L0_attn_P_v, L0_attn_P_o, L0_xattn_Wq, L0_xattn_bq, L0_xattn_Wk, L0_xattn_bk, L0_xattn_Wv, L0_xattn_bv, L0_xattn_Wo, L0_xattn_bo, L0_xattn_ln_gamma, L0_xattn_ln_beta, L0_ffn_w_gate, L0_ffn_w_up, L0_ffn_w_down):
    import jax
    import jax.numpy as jnp

    def _L0_attn_ref(x, P_q, P_k, P_v, P_o):
        import jax, jax.numpy as jnp
        import numpy as np
        import math
        D_K = 64
        m = x.shape[1]
        Q = jnp.einsum('bmd,hdk->bhmk', x, P_q)
        K = jnp.einsum('bmd,hdk->bhmk', x, P_k)
        V = jnp.einsum('bmd,hdv->bhmv', x, P_v)
        logits = jnp.einsum('bhmk,bhnk->bhmn', Q, K) * math.sqrt(D_K)
        causal = jnp.tril(jnp.ones((m, m), dtype=bool))
        logits = jnp.where(causal[None, None], logits, -jnp.inf)
        key_weights = jax.nn.softmax(logits, axis=-1)
        o = jnp.einsum('bhmm,bhmv->bhmv', key_weights, V)
        y = jnp.einsum('bhmv,hdv->bmd', o, P_o)
        return y

    def _L0_xattn_ref(query, key, value, Wq, bq, Wk, bk, Wv, bv, Wo, bo, ln_gamma, ln_beta):
        import jax, jax.numpy as jnp
        import numpy as np
        N_HEAD, MODEL_DIM, KEY_DIM, VALUE_DIM = (16, 128, 64, 64)
        B, S = (4, 256)
        EPS = 1e-05
        TEMP = float(np.sqrt(KEY_DIM))
        b, sq, _ = query.shape
        residual = query
        q = (query @ Wq + bq).reshape(b, sq, N_HEAD, KEY_DIM)
        k = (key @ Wk + bk).reshape(b, key.shape[1], N_HEAD, KEY_DIM)
        v = (value @ Wv + bv).reshape(b, value.shape[1], N_HEAD, VALUE_DIM)
        scores = jnp.einsum('bqhd,bkhd->bhqk', q, k) / TEMP
        attn = jax.nn.softmax(scores, axis=-1)
        out = jnp.einsum('bhqk,bkhd->bqhd', attn, v).reshape(b, sq, N_HEAD * VALUE_DIM)
        out = out @ Wo + bo + residual
        mu = jnp.mean(out, axis=-1, keepdims=True)
        var = jnp.var(out, axis=-1, keepdims=True)
        return (out - mu) * jax.lax.rsqrt(var + EPS) * ln_gamma + ln_beta

    def _L0_ffn_ref(x, w_gate, w_up, w_down):
        import jax, jax.numpy as jnp
        import numpy as np
        DIM = 128
        HIDDEN = 384
        SCALE = 1.0 / 127.0

        def _dequant(w_int, dtype):
            return w_int.astype(dtype) * jnp.asarray(SCALE, dtype)
        wg = _dequant(w_gate, x.dtype)
        wu = _dequant(w_up, x.dtype)
        wd = _dequant(w_down, x.dtype)
        gate = jnp.einsum('bsd,hd->bsh', x, wg)
        up = jnp.einsum('bsd,hd->bsh', x, wu)
        h = jax.nn.silu(gate) * up
        return jnp.einsum('bsh,dh->bsd', h, wd)
    x = x + _L0_attn_ref(_layernorm(x, axis=-1), L0_attn_P_q, L0_attn_P_k, L0_attn_P_v, L0_attn_P_o)
    x = x + _L0_xattn_ref(_layernorm(x, axis=-1), ctx_1024, ctx_1024, L0_xattn_Wq, L0_xattn_bq, L0_xattn_Wk, L0_xattn_bk, L0_xattn_Wv, L0_xattn_bv, L0_xattn_Wo, L0_xattn_bo, L0_xattn_ln_gamma, L0_xattn_ln_beta)
    x = x + _L0_ffn_ref(_layernorm(x, axis=-1), L0_ffn_w_gate, L0_ffn_w_up, L0_ffn_w_down)
    return x

_drawn_inputs = setup_inputs


def setup_inputs(seed=0):
    import zlib

    import numpy as np

    out = dict(_drawn_inputs(seed))
    spreads = {'L0_xattn_bq': (0.0, 0.293),
     'L0_xattn_bk': (0.0, 0.8),
     'L0_xattn_bv': (0.0, 0.1),
     'L0_xattn_bo': (0.0, 0.1),
     'L0_xattn_ln_gamma': (1.0, 0.2),
     'L0_xattn_ln_beta': (0.0, 0.1)}
    factors = {'L0_attn_P_q': 3.482, 'L0_attn_P_k': 3.318}
    for name, (base, spread) in spreads.items():
        noise = np.random.default_rng([zlib.crc32(name.encode()), seed]).standard_normal(out[name].shape)
        drawn = base * np.exp(spread * noise) if base else spread * noise
        out[name] = jnp.asarray(drawn.astype(out[name].dtype))
    for name, factor in factors.items():
        out[name] = (out[name] * factor).astype(out[name].dtype)
    return out
```

```python
from contextlib import ExitStack

import concourse.bass as bass
from concourse import mybir

ALU = mybir.AluOpType
ACT = mybir.ActivationFunctionType
AX = mybir.AxisListType
F32 = mybir.dt.float32
F32R = mybir.dt.float32r
BF16 = mybir.dt.bfloat16
I32 = mybir.dt.int32

EPS = 1e-5
MASKED = -1e30


def decoder_layer(nc, x, ctx_t, pq_t, pk_t, pv, po, wq_t, bq_t, wk_t, bk_t, wv, bv, wo, bo, gamma, beta,
                  w_gate_t, w_up_t, w_down_t, out):
    B, SQ, D = x.shape
    SK = ctx_t.shape[2]
    DK, H = pq_t.shape[0], pq_t.shape[1]
    HV = wv.shape[1]
    P = 128
    QT = SQ // P
    NP = H // 2
    NC = HV // P
    KT = -(-SK // P)
    KL = SK - (KT - 1) * P
    CH = 4
    CW = SK // CH
    CL = SK - (CH - 1) * CW
    SKP = SK + SK % 2
    HID = w_gate_t.shape[1]
    HT = HID // P
    TEMP = 1.0 / float(DK) ** 0.5
    SHARP = float(DK) ** 0.5
    NU = H * QT
    NJ = NP * QT
    TG = -(-KT // 4)
    NV = KT * 2

    with ExitStack() as ctx:
        def sb(name, shape, dt=F32):
            return ctx.enter_context(nc.sbuf_tensor(name, shape, dt))

        def pb(name, shape):
            return ctx.enter_context(nc.psum_tensor(name, shape, F32))

        def sem(name):
            return ctx.enter_context(nc.semaphore(name))

        w_pv = sb("w_pv", [P, HV])
        w_po = sb("w_po", [P, NC, D])
        w_wo = sb("w_wo", [P, NC, D])
        wv_hi = sb("wv_hi", [P, HV], F32R)
        wv_lo = sb("wv_lo", [P, HV], F32R)
        qk_self = sb("qk_self", [P, H, D])
        qk_cross = sb("qk_cross", [P, H, D])
        qbias = sb("qbias", [P, H])
        ub = sb("ub", [P, H])
        t0 = sb("t0", [P, H])
        bqs = sb("bqs", [DK, H])
        bks = sb("bks", [DK, H])
        bqk = sb("bqk", [DK, H])
        ones64 = sb("ones64", [DK, P])
        bv_all = sb("bv_all", [P, HV])
        bo_all = sb("bo_all", [P, D])
        gamma_all = sb("gamma_all", [P, D])
        beta_all = sb("beta_all", [P, D])
        gate_w = sb("gate_w", [P, HID])
        up_w = sb("up_w", [P, HID])
        down_w = sb("down_w", [P, HT, D])
        ident = sb("ident", [P, P])
        ident_b = sb("ident_b", [P, P], BF16)
        mask_b = sb("mask_b", [P, SQ], BF16)
        nhalf = sb("nhalf", [P, QT])

        x_in = sb("x_in", [P, QT, D])
        x1 = sb("x1", [P, QT, D])
        x2 = sb("x2", [P, QT, D])
        xn = sb("xn", [P, QT, D])
        xt = sb("xt", [P, SQ])
        spare = sb("spare", [P, 1])
        stats = sb("stats", [P, QT, 6])
        mv = sb("mv", [P, QT, 2])
        var = sb("var", [P, QT])
        rstd = sb("rstd", [P, QT])
        ctx_raw = sb("ctx_raw", [P, SKP])
        ctx_hi = sb("ctx_hi", [P, SKP], F32R)
        ctx_lo = sb("ctx_lo", [P, SKP], F32R)
        vals = sb("vals", [P, KT, HV])
        qs = sb("qs", [P, 2, 2 * SQ])
        es = sb("es", [P, 2, P + SQ])
        junk = sb("junk", [P, 2, QT, P])
        nmx = sb("nmx", [P, H, QT])
        nmx8 = sb("nmx8", [P, H, QT])
        sums_s = sb("sums_s", [P, QT, H])
        diag_s = sb("diag_s", [P, QT, H])
        rsum_s = sb("rsum_s", [P, QT, H])
        wdiag = sb("wdiag", [P, QT, H])
        o_self = sb("o_self", [P, HV])
        o_self_t = sb("o_self_t", [P, NC, P])
        tterm = sb("tterm", [P, QT, H])
        tterm8 = sb("tterm8", [P, QT, H])
        q_hi = sb("q_hi", [P, 2, 2 * SQ], F32R)
        q_lo = sb("q_lo", [P, 2, 2 * SQ], F32R)
        mx4 = sb("mx4", [P, CH])
        mx = sb("mx", [P, 1])
        nb = sb("nb", [P, 1])
        ebias = sb("ebias", [P, 2])
        probs = sb("probs", [P, 2, SK])
        sums = sb("sums", [P, 4, 2])
        sum1 = sb("sum1", [P, 2])
        rsum = sb("rsum", [P, 2])
        rwide = sb("rwide", [P, 2, DK])
        probs_t = sb("probs_t", [P, 2, 2, KT, P])
        rt = sb("rt", [P, P])
        attn_t = sb("attn_t", [P, NP, SQ])
        y = sb("y", [P, QT, D])
        h_e = sb("h_e", [P, HT, SQ])
        h_act = sb("h_act", [P, HT, SQ])
        fin = sb("fin", [P, QT, D])

        stage = vals[:, :, :].rearrange("p k v -> p (k v)")
        st_pq, st_pk, st_wq, st_wk = (
            stage[0:DK, i * H * D:(i + 1) * H * D].rearrange("p (h d) -> p h d", h=H) for i in range(4))
        w_wv = stage[:, 4 * H * D:4 * H * D + HV]
        ints = stage[:, 4 * H * D + HV:4 * H * D + HV + 3 * HID].bitcast(I32)
        gate_int, up_int = ints[:, 0:HID], ints[:, HID:2 * HID]
        down_int = ints[:, 2 * HID:3 * HID].rearrange("p (c d) -> p c d", c=HT)

        ps_s = pb("ps_s", [P, CH, 512])
        ps_t = [pb("ps_t0", [P, 512]), pb("ps_t1", [P, 512])]
        ps_o = pb("ps_o", [P, 512])
        ps_m = pb("ps_m", [P, 512])

        w_in = sem("w_in")
        x_got = sem("x_got")
        ctx_got = sem("ctx_got")
        out_put = sem("out_put")
        consts = sem("consts")
        fold_mm = sem("fold_mm")
        fold_cp = sem("fold_cp")
        prep = sem("prep")
        dve_step = sem("dve_step")
        wvhi_done = sem("wvhi_done")
        ctxhi_done = sem("ctxhi_done")
        ctxlo_done = sem("ctxlo_done")
        v_mm = sem("v_mm")
        v_cp = sem("v_cp")
        var_done = sem("var_done")
        rstd_done = sem("rstd_done")
        xn_done = sem("xn_done")
        xt_mm = sem("xt_mm")
        xt_cp = sem("xt_cp")
        qs_mm = sem("qs_mm")
        qs_cp = sem("qs_cp")
        logit_mm = sem("logit_mm")
        nmax_done = sem("nmax_done")
        es_done = sem("es_done")
        diag_done = sem("diag_done")
        vs_mm = sem("vs_mm")
        os_done = sem("os_done")
        ot_mm = sem("ot_mm")
        ot_cp = sem("ot_cp")
        ys_mm = sem("ys_mm")
        x1_done = sem("x1_done")
        t_mm = sem("t_mm")
        t_done = sem("t_done")
        q_mm = sem("q_mm")
        qhi_done = sem("qhi_done")
        qlo_done = sem("qlo_done")
        s_mm = sem("s_mm")
        ebias_done = sem("ebias_done")
        exp_done = sem("exp_done")
        pt_mm = sem("pt_mm")
        pt_act = sem("pt_act")
        pt_dve = sem("pt_dve")
        av_mm = sem("av_mm")
        rwide_done = sem("rwide_done")
        rt_mm = sem("rt_mm")
        rt_cp = sem("rt_cp")
        attn_done = sem("attn_done")
        y_mm = sem("y_mm")
        x2_done = sem("x2_done")
        ffn_mm = sem("ffn_mm")
        sig_done = sem("sig_done")
        hact_done = sem("hact_done")
        down_mm = sem("down_mm")
        fin_done = sem("fin_done")

        block = ctx.enter_context(nc.Block())
        N_LOADS = 18
        PRE_STEPS, BATCH_STEPS = 1, 164

        @block.sync
        def _(sp):
            loads = [
                (st_pq, pq_t), (st_pk, pk_t), (st_wq, wq_t), (st_wk, wk_t), (bqs[:, :], bq_t), (bks[:, :], bk_t),
                (w_wv, wv), (bv_all[:, :], bv.partition_broadcast(P)),
                (w_pv[:, :], pv), (w_po[:, :, :], po.rearrange("(c p) d -> p c d", p=P)),
                (w_wo[:, :, :], wo.rearrange("(c p) d -> p c d", p=P)),
                (bo_all[:, :], bo.partition_broadcast(P)),
                (gamma_all[:, :], gamma.partition_broadcast(P)), (beta_all[:, :], beta.partition_broadcast(P)),
                (gate_int, w_gate_t), (up_int, w_up_t),
                (down_int, w_down_t.rearrange("(c p) d -> p c d", p=P)),
            ]
            for dst, src in loads:
                sp.dma_start(dst, src).then_inc(w_in, 16)
            assert len(loads) == N_LOADS - 1
            with sp.Fori(0, B) as b:
                sp.wait_ge(x1_done, b + 1)
                sp.dma_start(x_in[:, :, :], x[b].rearrange("(t p) d -> p t d", p=P)).then_inc(x_got, 16)
                sp.wait_ge(ctxlo_done, b + 1)
                sp.dma_start(ctx_raw[:, 0:SK], ctx_t[b]).then_inc(ctx_got, 16)

        @block.gpsimd
        def _(pool):
            pool.memset(ident[:, :], 0.0).then_inc(consts, 1)
            pool.memset(mask_b[:, :], 0.0).then_inc(consts, 1)
            pool.memset(nhalf[:, :], -0.5)
            pool.memset(ones64[:, :], 1.0)
            pool.memset(ctx_raw[:, SK:SKP], 0.0)
            pool.wait_ge(consts, 2)
            pool.affine_select(out=ident[:, :], in_=ident[:, :], compare_op=ALU.not_equal, fill=1.0, base=0,
                               pattern=[[-1, P]], channel_multiplier=1).then_inc(consts, 1)
            pool.affine_select(out=mask_b[:, :], in_=mask_b[:, :], compare_op=ALU.is_ge, fill=MASKED, base=P,
                               pattern=[[-1, SQ]], channel_multiplier=1).then_inc(consts, 1)
            pool.wait_ge(consts, 4)
            pool.tensor_copy(ident_b[:, :], ident[:, :]).then_inc(consts, 1)
            with pool.Fori(0, B) as b:
                for k in range(4):
                    pool.wait_ge(var_done, b * 4 + (k + 1))
                    pool.tensor_tensor(rstd[:, :], var[:, :], nhalf[:, :], ALU.pow).then_inc(rstd_done, 1)

        @block.tensor
        def _(pe):
            pe.wait_ge(w_in, 16 * (N_LOADS - 1))
            pe.wait_ge(consts, 5)
            for g in range(8):
                wa, wb = (st_pq, st_pk) if g < 4 else (st_wq, st_wk)
                for j in range(4):
                    h = 4 * (g % 4) + j
                    if g >= 4 and j == 0:
                        pe.wait_ge(fold_cp, g - 3)
                    mm = pe.matmul(ps_s[:, g % 4, j * D:(j + 1) * D], wa[:, h, :], wb[:, h, :], start=True, stop=True)
                mm.then_inc(fold_mm, 1)
            for h in range(H):
                pe.matmul(ps_t[0][:, h:h + 1], st_wk[:, h, :], bqs[:, h:h + 1], start=True, stop=True)
                mm = pe.matmul(ps_t[1][:, h:h + 1], st_wq[:, h, :], bks[:, h:h + 1], start=True, stop=True)
            mm.then_inc(fold_mm, 1)
            pe.wait_ge(prep, 1)
            pe.matmul(ps_o[:, 0:H], ones64[:, :], bqk[:, :], start=True, stop=True).then_inc(fold_mm, 1)
            pe.wait_ge(fold_cp, 11)
            pe.wait_ge(prep, 2)
            pe.wait_ge(wvhi_done, 1)

            with pe.Fori(0, B) as b:
                pe.wait_ge(ctxhi_done, b + 1)
                pe.wait_ge(ctxlo_done, b + 2)
                for k in range(NV):
                    i, n = k // 2, k % 2
                    rows = P if i < KT - 1 else KL
                    keys, cols = slice(i * P, i * P + rows), slice(n * 512, n * 512 + 512)
                    if k >= 4:
                        pe.wait_ge(v_cp, b * NV + (k - 3))
                    else:
                        pe.wait_ge(fin_done, b + 1)
                    if i == KT - 1:
                        pass
                    dst = ps_s[0:rows, k % 4, :]
                    pe.matmul(dst, ctx_hi[:, keys], wv_hi[:, cols], start=True, stop=False)
                    pe.matmul(dst, ctx_hi[:, keys], wv_lo[:, cols], start=False, stop=False)
                    pe.matmul(dst, ctx_lo[:, keys], wv_hi[:, cols], start=False, stop=True).then_inc(v_mm, 1)

                def transpose_rows(k):
                    pe.wait_ge(xn_done, b * 3 + (k + 1))
                    for t in range(QT):
                        mm = pe.transpose(ps_m[:, t * P:(t + 1) * P], xn[:, t, :], ident[:, :])
                    mm.then_inc(xt_mm, 1)
                    pe.wait_ge(xt_cp, b * 3 + (k + 1))

                transpose_rows(0)

                def self_q(p):
                    for a in range(2):
                        mm = pe.matmul(ps_t[p % 2][:, a * SQ:(a + 1) * SQ], qk_self[:, 2 * p + a, :], xt[:, :],
                                       start=True, stop=True)
                    mm.then_inc(qs_mm, 1)

                self_q(0)
                pe.wait_ge(v_cp, b * NV + NV)
                for h in range(H):
                    if h % 2 == 0 and h // 2 + 1 < NP:
                        if h >= 2:
                            pe.wait_ge(qs_cp, b * NP + h // 2)
                        self_q(h // 2 + 1)
                    pe.wait_ge(qs_cp, b * NP + (h // 2 + 1))
                    if h >= 4:
                        pe.wait_ge(es_done, b * H + (h - 3))
                    q = qs[:, (h // 2) % 2, (h % 2) * SQ:(h % 2 + 1) * SQ]
                    bank = ps_s[:, h % 4, :]
                    pe.matmul(bank[:, 0:P], q[:, 0:P], xt[:, 0:P], start=True, stop=False)
                    pe.matmul(bank[:, 0:P], ident_b[:, :], mask_b[:, P:SQ], start=False, stop=True)
                    pe.matmul(bank[:, P:P + SQ], q[:, P:SQ], xt[:, :], start=True, stop=False)
                    pe.matmul(bank[:, P:P + SQ], ident_b[:, :], mask_b[:, :], start=False,
                              stop=True).then_inc(logit_mm, 1)
                for t in range(QT):
                    if t == 0:
                        pe.wait_ge(qs_cp, b * NP + NP)
                    else:
                        pe.wait_ge(os_done, b * QT + t)
                    for n in range(2):
                        mm = pe.matmul(ps_t[n][:, :], xt[:, t * P:(t + 1) * P], w_pv[:, n * 512:(n + 1) * 512],
                                       start=True, stop=True)
                    mm.then_inc(vs_mm, 1)
                    pe.wait_ge(os_done, b * QT + (t + 1))
                    if t == 0:
                        pe.wait_ge(es_done, b * H + H)
                    else:
                        pe.wait_ge(ot_cp, b * QT + t)
                    for c in range(NC):
                        mm = pe.transpose(ps_s[:, c // 4, (c % 4) * P:(c % 4 + 1) * P],
                                          o_self[:, c * P:(c + 1) * P], ident[:, :])
                    mm.then_inc(ot_mm, 1)
                    pe.wait_ge(ot_cp, b * QT + (t + 1))
                    for c in range(NC):
                        mm = pe.matmul(ps_o[:, t * P:(t + 1) * P], o_self_t[:, c, :], w_po[:, c, :],
                                       start=(c == 0), stop=(c == NC - 1))
                mm.then_inc(ys_mm, 1)

                transpose_rows(1)
                for t in range(QT):
                    mm = pe.matmul(ps_o[:, t * H:(t + 1) * H], xt[:, t * P:(t + 1) * P], ub[:, :],
                                   start=True, stop=True)
                mm.then_inc(t_mm, 1)

                def cross_q(p):
                    for a in range(2):
                        mm = pe.matmul(ps_m[:, a * SQ:(a + 1) * SQ], qk_cross[:, 2 * p + a, :], xt[:, :],
                                       start=True, stop=True)
                    mm.then_inc(q_mm, 1)

                def scores(u):
                    p, t, a = u // 4, u // 2 % 2, u % 2
                    at = a * SQ + t * P
                    hi, lo = q_hi[:, p % 2, at:at + P], q_lo[:, p % 2, at:at + P]
                    pe.wait_ge(qhi_done, b * NP + (p + 1))
                    pe.wait_ge(qlo_done, b * NP + (p + 1))
                    if u >= 1:
                        pe.wait_ge(exp_done, b * NU + u)
                    for c in range(CH):
                        n = CW if c < CH - 1 else SKP - (CH - 1) * CW
                        keys, dst = slice(c * CW, c * CW + n), ps_s[:, c, 0:n]
                        pe.matmul(dst, hi, ctx_hi[:, keys], start=True, stop=False)
                        pe.matmul(dst, hi, ctx_lo[:, keys], start=False, stop=False)
                        pe.matmul(dst, lo, ctx_hi[:, keys], start=False, stop=True).then_inc(s_mm, 1)

                def transposes(u):
                    pe.wait_ge(exp_done, b * NU + (u + 1))
                    for g in range(TG):
                        if u == 0 and g < 2:
                            pass
                        elif g % 2 == 0:
                            pe.wait_ge(pt_act, b * NU * 2 + (2 * u + g // 2))
                        else:
                            pe.wait_ge(pt_dve, b * NU * 2 + (2 * u + g // 2))
                        for i in range(4 * g, min(4 * g + 4, KT)):
                            n = P if i < KT - 1 else KL
                            mm = pe.transpose(ps_t[g % 2][0:n, (i % 4) * P:(i % 4 + 1) * P],
                                              probs[:, u % 2, i * P:i * P + n], ident[:, :])
                        mm.then_inc(pt_mm, 1)

                def weigh(j):
                    p, t = j // QT, j % QT
                    pe.wait_ge(pt_act, b * NU * 2 + 4 * (j + 1))
                    pe.wait_ge(pt_dve, b * NU * 2 + 4 * (j + 1))
                    if j == 0:
                        pe.wait_ge(t_done, b + 1)
                    else:
                        pe.wait_ge(attn_done, b * NJ + j)
                    for i in range(KT):
                        rows = P if i < KT - 1 else KL
                        for a in range(2):
                            at = (2 * p + a) * DK
                            mm = pe.matmul(ps_o[a * DK:(a + 1) * DK, 0:P], vals[0:rows, i, at:at + DK],
                                           probs_t[0:rows, j % 2, a, i, :], start=(i == 0), stop=(i == KT - 1),
                                           skip_group_check=True)
                    mm.then_inc(av_mm, 1)
                    pe.wait_ge(rwide_done, b * NJ + (j + 1))
                    if j > 0:
                        pe.wait_ge(rt_cp, b * NJ + j)
                    pe.wait_ge(qlo_done, b * NP + min((2 * j + 2) // 4 + 1, NP))
                    pe.transpose(ps_m[:, 0:P], rwide[:, :, :].rearrange("p a k -> p (a k)"),
                                 ident[:, :]).then_inc(rt_mm, 1)

                cross_q(0)
                scores(0)
                for u in range(NU):
                    if u + 1 < NU:
                        scores(u + 1)
                    transposes(u)
                    if u % 2 == 0 and u > 0:
                        weigh(u // 2 - 1)
                    if u % 4 == 1 and u // 4 + 1 < NP:
                        if u > 4:
                            pe.wait_ge(rt_cp, b * NJ + (u // 2))
                        cross_q(u // 4 + 1)
                weigh(NJ - 1)
                pe.wait_ge(attn_done, b * NJ + NJ)
                for t in range(QT):
                    for c in range(NP):
                        mm = pe.matmul(ps_o[:, t * P:(t + 1) * P], attn_t[:, c, t * P:(t + 1) * P], w_wo[:, c, :],
                                       start=(c == 0), stop=(c == NP - 1))
                mm.then_inc(y_mm, 1)

                transpose_rows(2)
                for c in range(HT):
                    pe.matmul(ps_s[:, c, 0:SQ], gate_w[:, c * P:(c + 1) * P], xt[:, :], start=True, stop=True)
                    mm = pe.matmul(ps_s[:, c, SQ:2 * SQ], up_w[:, c * P:(c + 1) * P], xt[:, :], start=True, stop=True)
                mm.then_inc(ffn_mm, 1)
                pe.wait_ge(hact_done, b + 1)
                for t in range(QT):
                    for c in range(HT):
                        mm = pe.matmul(ps_o[:, t * P:(t + 1) * P], h_act[:, c, t * P:(t + 1) * P], down_w[:, c, :],
                                       start=(c == 0), stop=(c == HT - 1))
                mm.then_inc(down_mm, 1)

        @block.scalar
        def _(act):
            act.wait_ge(w_in, 16 * (N_LOADS - 1))
            act.activation(wv_hi[:, :], w_wv, ACT.Copy).then_inc(wvhi_done, 1)
            with act.Fori(0, B) as b:
                act.wait_ge(ctx_got, b * 16 + 16)
                act.wait_ge(consts, 5)
                act.wait_ge(fin_done, b + 1)
                act.activation(ctx_hi[:, :], ctx_raw[:, :], ACT.Copy).then_inc(ctxhi_done, 1)

                def copy_rows(k):
                    act.wait_ge(xt_mm, b * 3 + (k + 1))
                    act.activation(xt[:, :], ps_m[:, 0:SQ], ACT.Copy).then_inc(xt_cp, 1)

                copy_rows(0)

                def self_q(p):
                    act.wait_ge(qs_mm, b * NP + (p + 1))
                    if p >= 2:
                        act.wait_ge(logit_mm, b * H + 2 * (p - 1))
                    act.activation(qs[:, p % 2, :], ps_t[p % 2][:, :], ACT.Copy).then_inc(qs_cp, 1)

                self_q(0)
                for h in range(H):
                    if h % 2 == 0 and h // 2 + 1 < NP:
                        self_q(h // 2 + 1)
                    act.wait_ge(nmax_done, b * H + (h + 1))
                    if h >= 2:
                        act.wait_ge(diag_done, b * H + (h - 1))
                    for t in range(QT):
                        lo, n = t * P, (t + 1) * P
                        ins = act.activation(es[:, h % 2, lo:lo + n], ps_s[:, h % 4, lo:lo + n], ACT.Exp,
                                             bias=nmx8[:, h, t:t + 1], scale=SHARP, accum_out=sums_s[:, t, h:h + 1])
                    ins.then_inc(es_done, 1)
                for t in range(QT):
                    act.wait_ge(ot_mm, b * QT + (t + 1))
                    if t > 0:
                        pass
                    act.activation(o_self_t[:, :, :], ps_s[:, 0:2, :].rearrange("p b (c n) -> p (b c) n", n=P),
                                   ACT.Copy).then_inc(ot_cp, 1)

                copy_rows(1)

                def cross_q_hi(p):
                    act.wait_ge(q_mm, b * NP + (p + 1))
                    for a in range(2):
                        ins = act.activation(q_hi[:, p % 2, a * SQ:(a + 1) * SQ], ps_m[:, a * SQ:(a + 1) * SQ],
                                             ACT.Identity, bias=qbias[:, 2 * p + a:2 * p + a + 1])
                    ins.then_inc(qhi_done, 1)

                def exps(u):
                    act.wait_ge(ebias_done, b * NU + (u + 1))
                    if u >= 2:
                        act.wait_ge(pt_mm, b * NU * TG + TG * (u - 1))
                    n = (CH - 1) * CW
                    act.activation(probs[:, u % 2, 0:n].rearrange("p (c k) -> p c k", c=CH - 1),
                                   ps_s[:, 0:CH - 1, 0:CW], ACT.Exp, bias=ebias[:, u % 2:u % 2 + 1], scale=TEMP,
                                   accum_out=sums[:, u % 4, 0:1])
                    act.activation(probs[:, u % 2, n:SK], ps_s[:, CH - 1, 0:CL], ACT.Exp,
                                   bias=ebias[:, u % 2:u % 2 + 1], scale=TEMP,
                                   accum_out=sums[:, u % 4, 1:2]).then_inc(exp_done, 1)

                def copy_group(u, g):
                    j, a = u // 2, u % 2
                    act.wait_ge(pt_mm, b * NU * TG + (TG * u + g + 1))
                    if g == 0 and j >= 2:
                        act.wait_ge(av_mm, b * NJ + (j - 1))
                    n = min(4, KT - 4 * g)
                    act.activation(probs_t[:, j % 2, a, 4 * g:4 * g + n, :],
                                   ps_t[0][:, 0:n * P].rearrange("p (i q) -> p i q", q=P),
                                   ACT.Copy).then_inc(pt_act, 1)

                cross_q_hi(0)
                exps(0)
                for u in range(NU):
                    copy_group(u, 0)
                    if u + 1 < NU:
                        exps(u + 1)
                    copy_group(u, 2)
                    if u % 2 == 0 and u > 0:
                        act.wait_ge(rt_mm, b * NJ + u // 2)
                        if u > 2:
                            act.wait_ge(attn_done, b * NJ + (u // 2 - 1))
                        act.activation(rt[:, :], ps_m[:, 0:P], ACT.Copy).then_inc(rt_cp, 1)
                    if u % 4 == 1 and u // 4 + 1 < NP:
                        cross_q_hi(u // 4 + 1)
                act.wait_ge(rt_mm, b * NJ + NJ)
                act.wait_ge(attn_done, b * NJ + (NJ - 1))
                act.activation(rt[:, :], ps_m[:, 0:P], ACT.Copy).then_inc(rt_cp, 1)

                copy_rows(2)
                act.wait_ge(ffn_mm, b + 1)
                act.activation(h_e[:, :, :], ps_s[:, 0:HT, 0:SQ], ACT.Exp, scale=-1.0).then_inc(sig_done, 1)
                act.wait_ge(fin_done, b + 2)
                act.dma_start(out[b].rearrange("(t p) d -> p t d", p=P), fin[:, :, :]).then_inc(out_put, 16)
                act.wait_ge(out_put, b * 16 + 16)

        @block.vector
        def _(dve):
            dve.wait_ge(w_in, 16 * (N_LOADS - 1))
            steps = [0]

            def then(ins):
                steps[0] += 1
                ins.then_inc(dve_step, 1)
                if steps[0] <= PRE_STEPS:
                    dve.wait_ge(dve_step, steps[0])
                else:
                    dve.wait_ge(dve_step, b * BATCH_STEPS + steps[0])

            dve.tensor_tensor(bqk[:, :], bqs[:, :], bks[:, :], ALU.mult).then_inc(prep, 1)
            dve.memset(spare[:, :], 0.0).then_inc(x1_done, 1)
            dve.tensor_scalar(gate_w[:, :], gate_int, 1.0 / 127.0, None, ALU.mult).then_inc(fin_done, 1)
            dve.tensor_scalar(up_w[:, :], up_int, 1.0 / 127.0, None, ALU.mult).then_inc(ctxlo_done, 1)
            then(dve.tensor_scalar(down_w[:, :, :], down_int, 1.0 / 127.0, None, ALU.mult))
            dve.wait_ge(wvhi_done, 1)
            dve.tensor_tensor(wv_lo[:, :], w_wv, wv_hi[:, :].bitcast(F32), ALU.subtract).then_inc(prep, 1)
            for g in range(8):
                dst = qk_self if g < 4 else qk_cross
                dve.wait_ge(fold_mm, g + 1)
                dve.tensor_copy(dst[:, 4 * (g % 4):4 * (g % 4) + 4, :],
                                ps_s[:, g % 4, :].rearrange("p (h d) -> p h d", h=4)).then_inc(fold_cp, 1)
            dve.wait_ge(fold_mm, 9)
            dve.tensor_copy(qbias[:, :], ps_t[0][:, 0:H]).then_inc(fold_cp, 1)
            dve.tensor_copy(ub[:, :], ps_t[1][:, 0:H]).then_inc(fold_cp, 1)
            dve.wait_ge(fold_mm, 10)
            dve.tensor_copy(t0[:, :], ps_o[:, 0:H]).then_inc(fold_cp, 1)

            with dve.Fori(0, B) as b:
                def normalise(k, src, dst):
                    for t in range(QT):
                        ins = dve.bn_stats(stats[:, t, :], src[:, t, :])
                    then(ins)
                    dve.memset(spare[:, :], 0.0)
                    for t in range(QT):
                        ins = dve.bn_aggr(mv[:, t, :], stats[:, t, :])
                    then(ins)
                    dve.tensor_scalar(var[:, :], mv[:, :, 1], EPS, None, ALU.add).then_inc(var_done, 1)
                    dve.wait_ge(rstd_done, b * 4 + (k + 1))
                    for t in range(QT):
                        ins = dve.tensor_scalar(dst[:, t, :], src[:, t, :], mv[:, t, 0:1], rstd[:, t:t + 1],
                                                ALU.subtract, ALU.mult)
                    return ins

                dve.wait_ge(x_got, b * 16 + 16)
                normalise(0, x_in, xn).then_inc(xn_done, 1)
                dve.wait_ge(ctxhi_done, b + 1)
                dve.tensor_tensor(ctx_lo[:, :], ctx_raw[:, :], ctx_hi[:, :].bitcast(F32),
                                  ALU.subtract).then_inc(ctxlo_done, 1)
                for k in range(NV):
                    i, n = k // 2, k % 2
                    rows = P if i < KT - 1 else KL
                    dve.wait_ge(v_mm, b * NV + (k + 1))
                    dve.tensor_tensor(vals[0:rows, i, n * 512:(n + 1) * 512], ps_s[0:rows, k % 4, :],
                                      bv_all[0:rows, n * 512:(n + 1) * 512], ALU.add).then_inc(v_cp, 1)

                def diagonal(h):
                    dve.wait_ge(es_done, b * H + (h + 1))
                    for t in range(QT):
                        ins = dve.scalar_tensor_tensor(out=junk[:, h % 2, t, :], in0=es[:, h % 2, 2 * t * P:(2 * t + 1) * P],
                                                       scalar=1.0, in1=ident[:, :], op0=ALU.mult, op1=ALU.mult,
                                                       accum_out=diag_s[:, t, h:h + 1])
                    ins.then_inc(diag_done, 1)

                for h in range(H):
                    dve.wait_ge(logit_mm, b * H + (h + 1))
                    for t in range(QT):
                        lo, n = t * P, (t + 1) * P
                        ins = dve.tensor_reduce(nmx[:, h, t:t + 1], ps_s[:, h % 4, lo:lo + n], AX.X, ALU.max,
                                                negate=True)
                    then(ins)
                    dve.tensor_scalar(nmx8[:, h, :], nmx[:, h, :], SHARP, None, ALU.mult).then_inc(nmax_done, 1)
                    if h > 0:
                        diagonal(h - 1)
                diagonal(H - 1)
                then(dve.reciprocal(rsum_s[:, :, :], sums_s[:, :, :]))
                dve.wait_ge(diag_done, b * H + H)
                then(dve.tensor_tensor(wdiag[:, :, :], diag_s[:, :, :], rsum_s[:, :, :], ALU.mult))
                for t in range(QT):
                    dve.wait_ge(vs_mm, b * QT + (t + 1))
                    if t > 0:
                        dve.wait_ge(ot_mm, b * QT + t)
                    for n in range(2):
                        w = wdiag[:, t, 8 * n:8 * n + 8].unsqueeze(2).broadcast_to([P, 8, DK])
                        ins = dve.tensor_tensor(o_self[:, n * 512:(n + 1) * 512].rearrange("p (h k) -> p h k", k=DK),
                                                ps_t[n][:, :].rearrange("p (h k) -> p h k", k=DK), w, ALU.mult)
                    ins.then_inc(os_done, 1)
                dve.wait_ge(ys_mm, b + 1)
                ins = dve.tensor_tensor(x1[:, :, :], ps_o[:, 0:SQ].rearrange("p (t d) -> p t d", d=D), x_in[:, :, :],
                                        ALU.add)
                ins.then_inc(x1_done, 1)
                dve.wait_ge(x1_done, b + 2)
                normalise(1, x1, xn).then_inc(xn_done, 1)

                dve.wait_ge(t_mm, b + 1)
                for t in range(QT):
                    ins = dve.tensor_tensor(tterm[:, t, :], ps_o[:, t * H:(t + 1) * H], t0[:, :], ALU.add)
                then(ins)
                dve.tensor_scalar(tterm8[:, :, :], tterm[:, :, :], TEMP, None, ALU.mult).then_inc(t_done, 1)
                dve.wait_ge(t_done, b + 1)

                def cross_q_lo(p):
                    dve.wait_ge(qhi_done, b * NP + (p + 1))
                    for a in range(2):
                        cols = slice(a * SQ, (a + 1) * SQ)
                        ins = dve.scalar_tensor_tensor(out=q_lo[:, p % 2, cols], in0=ps_m[:, cols],
                                                       scalar=qbias[:, 2 * p + a:2 * p + a + 1],
                                                       in1=q_hi[:, p % 2, cols].bitcast(F32),
                                                       op0=ALU.add, op1=ALU.subtract)
                    ins.then_inc(qlo_done, 1)

                def maxima(u):
                    h, t = 2 * (u // 4) + u % 2, u // 2 % 2
                    for c in range(CH):
                        dve.wait_ge(s_mm, b * NU * CH + (CH * u + c + 1))
                        ins = dve.tensor_reduce(mx4[:, c:c + 1], ps_s[:, c, 0:CW if c < CH - 1 else CL], AX.X, ALU.max)
                    then(ins)
                    then(dve.tensor_reduce(mx[:, :], mx4[:, :], AX.X, ALU.max))
                    then(dve.tensor_scalar(nb[:, :], mx[:, :], tterm[:, t, h:h + 1], -TEMP, ALU.add, ALU.mult))
                    if u >= 2:
                        dve.wait_ge(exp_done, b * NU + (u - 1))
                    dve.tensor_tensor(ebias[:, u % 2:u % 2 + 1], nb[:, :], tterm8[:, t, h:h + 1],
                                      ALU.add).then_inc(ebias_done, 1)

                def copy_group(u, g):
                    j, a = u // 2, u % 2
                    dve.wait_ge(pt_mm, b * NU * TG + (TG * u + g + 1))
                    if g == 1 and j >= 2:
                        dve.wait_ge(av_mm, b * NJ + (j - 1))
                    n = min(4, KT - 4 * g)
                    rows = P if g < TG - 1 else KL
                    dve.tensor_copy(probs_t[0:rows, j % 2, a, 4 * g:4 * g + n, :],
                                    ps_t[1][0:rows, 0:n * P].rearrange("p (i q) -> p i q", q=P)).then_inc(pt_dve, 1)

                def weights_wide(j):
                    s0 = 2 * (j % 2)
                    dve.wait_ge(exp_done, b * NU + (2 * j + 2))
                    then(dve.tensor_tensor(sum1[:, :], sums[:, s0:s0 + 2, 0], sums[:, s0:s0 + 2, 1], ALU.add))
                    then(dve.reciprocal(rsum[:, :], sum1[:, :]))
                    if j > 0:
                        dve.wait_ge(rt_mm, b * NJ + j)
                    dve.tensor_copy(rwide[:, :, :], rsum[:, :].unsqueeze(2).broadcast_to([P, 2, DK])).then_inc(rwide_done, 1)

                def normal_out(j):
                    p, t = j // QT, j % QT
                    dve.wait_ge(rt_cp, b * NJ + (j + 1))
                    dve.wait_ge(av_mm, b * NJ + (j + 1))
                    dve.tensor_tensor(attn_t[:, p, t * P:(t + 1) * P], ps_o[:, 0:P], rt[:, :],
                                      ALU.mult).then_inc(attn_done, 1)

                cross_q_lo(0)
                maxima(0)
                for u in range(NU):
                    if u + 1 < NU:
                        maxima(u + 1)
                    copy_group(u, 1)
                    copy_group(u, 3)
                    if u % 2 == 1:
                        weights_wide(u // 2)
                    if u % 2 == 0 and u > 0:
                        normal_out(u // 2 - 1)
                    if u % 4 == 1 and u // 4 + 1 < NP:
                        cross_q_lo(u // 4 + 1)
                normal_out(NJ - 1)

                dve.wait_ge(y_mm, b + 1)
                for t in range(QT):
                    ins = dve.tensor_tensor(y[:, t, :], ps_o[:, t * P:(t + 1) * P], bo_all[:, :], ALU.add)
                then(ins)
                then(dve.tensor_tensor(y[:, :, :], y[:, :, :], xn[:, :, :], ALU.add))
                then(normalise(2, y, y))
                for t in range(QT):
                    ins = dve.tensor_tensor(y[:, t, :], y[:, t, :], gamma_all[:, :], ALU.mult)
                then(ins)
                for t in range(QT):
                    ins = dve.tensor_tensor(y[:, t, :], y[:, t, :], beta_all[:, :], ALU.add)
                then(ins)
                then(dve.tensor_tensor(x2[:, :, :], x1[:, :, :], y[:, :, :], ALU.add))
                normalise(3, x2, xn).then_inc(xn_done, 1)

                dve.wait_ge(sig_done, b + 1)
                then(dve.tensor_scalar(h_e[:, :, :], h_e[:, :, :], 1.0, None, ALU.add))
                then(dve.reciprocal(h_e[:, :, :], h_e[:, :, :]))
                then(dve.tensor_tensor(h_e[:, :, :], ps_s[:, 0:HT, 0:SQ], h_e[:, :, :], ALU.mult))
                dve.tensor_tensor(h_act[:, :, :], ps_s[:, 0:HT, SQ:2 * SQ], h_e[:, :, :], ALU.mult).then_inc(hact_done, 1)
                dve.wait_ge(down_mm, b + 1)
                dve.tensor_tensor(fin[:, :, :], ps_o[:, 0:SQ].rearrange("p (t d) -> p t d", d=D), x2[:, :, :],
                                  ALU.add).then_inc(fin_done, 1)
            assert steps[0] == PRE_STEPS + BATCH_STEPS


def kernel(**inputs):
    import numpy as np
    import concourse.bacc as bacc
    from concourse.bass_utils import run_bass_kernel_spmd

    a = {k: np.asarray(v) for k, v in inputs.items()}

    def heads_last(w):
        return w.transpose(2, 0, 1)

    def by_head(w):
        return w.reshape(w.shape[0], -1, 64).transpose(2, 1, 0)

    laid = {
        "x": a["x"],
        "ctx_t": a["ctx_1024"].transpose(0, 2, 1),
        "pq_t": heads_last(a["L0_attn_P_q"]),
        "pk_t": heads_last(a["L0_attn_P_k"]),
        "pv": a["L0_attn_P_v"].transpose(1, 0, 2).reshape(128, -1),
        "po": a["L0_attn_P_o"].transpose(0, 2, 1).reshape(-1, 128),
        "wq_t": by_head(a["L0_xattn_Wq"]),
        "bq_t": a["L0_xattn_bq"].reshape(-1, 64).T,
        "wk_t": by_head(a["L0_xattn_Wk"]),
        "bk_t": a["L0_xattn_bk"].reshape(-1, 64).T,
        "wv": a["L0_xattn_Wv"],
        "bv": a["L0_xattn_bv"],
        "wo": a["L0_xattn_Wo"],
        "bo": a["L0_xattn_bo"],
        "gamma": a["L0_xattn_ln_gamma"],
        "beta": a["L0_xattn_ln_beta"],
        "w_gate_t": a["L0_ffn_w_gate"].T,
        "w_up_t": a["L0_ffn_w_up"].T,
        "w_down_t": a["L0_ffn_w_down"].T,
    }
    nc = bacc.Bacc("TRN2", target_bir_lowering=False, num_devices=1)
    arrays, args = {}, []
    for name, v in laid.items():
        v = np.ascontiguousarray(v)
        arrays[f"in_{name}"] = v
        args.append(nc.dram_tensor(f"in_{name}", v.shape, mybir.dt.from_np(v.dtype), kind="ExternalInput").ap())
    out = nc.dram_tensor("out_x", a["x"].shape, F32, kind="ExternalOutput").ap()
    decoder_layer(nc, *args, out)
    r = run_bass_kernel_spmd(nc, [arrays], core_ids=[0])
    return r.results[0]["out_x"]
```

```python
from contextlib import ExitStack

import concourse.bass as bass
from concourse import mybir

ALU = mybir.AluOpType
ACT = mybir.ActivationFunctionType
AX = mybir.AxisListType
F32 = mybir.dt.float32
F32R = mybir.dt.float32r
BF16 = mybir.dt.bfloat16
I32 = mybir.dt.int32

EPS = 1e-5
MASKED = -1e30


def decoder_layer(nc, x, ctx_t, pq_t, pk_t, pv, po, wq_t, wk_t, wq, wk, bq, bk, wv, bv, wo, bo, gamma, beta,
                  w_gate_t, w_up_t, w_down_t, out):
    B, SQ, D = x.shape
    SK = ctx_t.shape[2]
    DK, H = pq_t.shape[0], pq_t.shape[1]
    HV = wv.shape[1]
    P = 128
    QT = SQ // P
    NP = H // 2
    NC = HV // P
    KT = -(-SK // P)
    KL = SK - (KT - 1) * P
    CH = 4
    CW = SK // CH
    CL = SK - (CH - 1) * CW
    SKP = SK + SK % 2
    HID = w_gate_t.shape[1]
    HT = HID // P
    TEMP = 1.0 / float(DK) ** 0.5
    SHARP = float(DK) ** 0.5
    NU = H * QT
    NJ = NP * QT
    TG = -(-KT // 4)
    N_REST = 10
    NV = KT * 2

    with ExitStack() as ctx:
        def sb(name, shape, dt=F32):
            return ctx.enter_context(nc.sbuf_tensor(name, shape, dt))

        def pb(name, shape):
            return ctx.enter_context(nc.psum_tensor(name, shape, F32))

        def sem(name):
            return ctx.enter_context(nc.semaphore(name))

        w_pv = sb("w_pv", [P, HV])
        w_po = sb("w_po", [P, NC, D])
        w_wo = sb("w_wo", [P, NC, D])
        wv_hi = sb("wv_hi", [P, HV], F32R)
        wv_lo = sb("wv_lo", [P, HV], F32R)
        qk_self = sb("qk_self", [P, H, D])
        qk_cross = sb("qk_cross", [P, H, D])
        qbias = sb("qbias", [P, H])
        ub = sb("ub", [P, H])
        t0 = sb("t0", [P, H])
        bv_c = sb("bv_c", [P, NC])
        bo_in = sb("bo_in", [P, D])
        bo_all = sb("bo_all", [P, D])
        gamma_all = sb("gamma_all", [P, D])
        beta_all = sb("beta_all", [P, D])
        gate_w = sb("gate_w", [P, HID])
        up_w = sb("up_w", [P, HID])
        down_w = sb("down_w", [P, HT, D])
        ident = sb("ident", [P, P])
        ident_b = sb("ident_b", [P, P], BF16)
        mask_b = sb("mask_b", [P, SQ], BF16)
        nhalf = sb("nhalf", [P, QT])

        x_in = sb("x_in", [P, QT, D])
        x1 = sb("x1", [P, QT, D])
        x2 = sb("x2", [P, QT, D])
        xn = [sb(f"xn{k}", [P, QT, D]) for k in range(3)]
        xt = [sb(f"xt{k}", [P, SQ]) for k in range(3)]
        spare = sb("spare", [P, 1])
        stats = sb("stats", [P, QT, 6])
        mv = sb("mv", [P, QT, 2])
        var = sb("var", [P, QT])
        rstd = sb("rstd", [P, QT])
        ctx_raw = sb("ctx_raw", [P, SKP])
        ctx_hi = sb("ctx_hi", [P, SKP], F32R)
        ctx_lo = sb("ctx_lo", [P, SKP], F32R)
        vals = sb("vals", [P, KT, HV])
        qs = sb("qs", [P, 2, 2 * SQ])
        es = sb("es", [P, 2, P + SQ])
        junk = sb("junk", [P, 2, QT, P])
        nmx = sb("nmx", [P, H, QT])
        nmx8 = sb("nmx8", [P, H, QT])
        sums_s = sb("sums_s", [P, QT, H])
        diag_s = sb("diag_s", [P, QT, H])
        rsum_s = sb("rsum_s", [P, QT, H])
        wdiag = sb("wdiag", [P, QT, H])
        o_self_t = sb("o_self_t", [P, NC, P])
        tterm = sb("tterm", [P, QT, H])
        tterm8 = sb("tterm8", [P, QT, H])
        q_hi = sb("q_hi", [P, 2, 2 * SQ], F32R)
        q_lo = sb("q_lo", [P, 2, 2 * SQ], F32R)
        mx4 = sb("mx4", [P, CH])
        mx3 = sb("mx3", [P, 1])
        nb = sb("nb", [P, 1])
        ebias = sb("ebias", [P, 2])
        probs = sb("probs", [P, 2, SK])
        sums = sb("sums", [P, 8, 3])
        sum1 = sb("sum1", [P, 2])
        rsum = sb("rsum", [P, 2])
        rwide = sb("rwide", [P, 2, DK])
        o_self = probs[:, :, 0:HV]
        probs_t = sb("probs_t", [P, 2, 2, KT, P])
        wide_wq, wide_wk, wide_bq, wide_bk = (
            probs_t[:, :, :, :, :].rearrange("p j a i q -> p (j a i q)")[:, i * HV:(i + 1) * HV] for i in range(4))
        rt = sb("rt", [P, P])
        attn_t = sb("attn_t", [P, NP, SQ])
        y = sb("y", [P, QT, D])
        h_e = sb("h_e", [P, HT, SQ])
        h_act = sb("h_act", [P, HT, SQ])
        fin = sb("fin", [P, QT, D])

        stage = vals[:, :, :].rearrange("p k v -> p (k v)")
        st_pq, st_pk, st_wq, st_wk = (
            stage[0:DK, i * H * D:(i + 1) * H * D].rearrange("p (h d) -> p h d", h=H) for i in range(4))
        w_wv = stage[:, 4 * H * D:4 * H * D + HV]
        ints = stage[:, 4 * H * D + HV:4 * H * D + HV + 3 * HID].bitcast(I32)
        gate_int, up_int = ints[:, 0:HID], ints[:, HID:2 * HID]
        down_int = ints[:, 2 * HID:3 * HID].rearrange("p (c d) -> p c d", c=HT)
        bv_wide = stage[:, 4 * H * D + HV + 3 * HID:4 * H * D + 2 * HV + 3 * HID].rearrange("p (c n) -> p c n", c=NC)

        ps_s = pb("ps_s", [P, CH, 512])
        ps_t = [pb("ps_t0", [P, 512]), pb("ps_t1", [P, 512])]
        ps_o = pb("ps_o", [P, 512])
        ps_m = pb("ps_m", [P, 512])
        ps_h = [ps_o, ps_m]

        w_self = sem("w_self")
        w_cross = sem("w_cross")
        w_bias = sem("w_bias")
        bias_mul = sem("bias_mul")
        w_in = sem("w_in")
        x_got = sem("x_got")
        ctx_got = sem("ctx_got")
        out_put = sem("out_put")
        consts = sem("consts")
        fold_mm = sem("fold_mm")
        bias_done = sem("bias_done")
        fold_cp = sem("fold_cp")
        prep = sem("prep")
        dve_step = sem("dve_step")
        wvhi_done = sem("wvhi_done")
        ctxhi_done = sem("ctxhi_done")
        ctxlo_done = sem("ctxlo_done")
        v_mm = sem("v_mm")
        v_cp = sem("v_cp")
        var_done = sem("var_done")
        rstd_done = sem("rstd_done")
        xn_done = [sem(f"xn_done{k}") for k in range(3)]
        xt_mm = [sem(f"xt_mm{k}") for k in range(3)]
        xt_cp = [sem(f"xt_cp{k}") for k in range(3)]
        qs_mm = sem("qs_mm")
        qs_cp = sem("qs_cp")
        logit_mm = sem("logit_mm")
        nmax_done = sem("nmax_done")
        es_done = sem("es_done")
        diag_done = sem("diag_done")
        vs_mm = sem("vs_mm")
        os_done = sem("os_done")
        ot_mm = sem("ot_mm")
        ot_cp = sem("ot_cp")
        ys_mm = sem("ys_mm")
        x1_done = sem("x1_done")
        t_mm = sem("t_mm")
        t_done = sem("t_done")
        q_mm = sem("q_mm")
        qhi_done = sem("qhi_done")
        qlo_done = sem("qlo_done")
        s_mm = sem("s_mm")
        ebias_done = sem("ebias_done")
        exp_done = sem("exp_done")
        pt_mm = sem("pt_mm")
        pt_act = sem("pt_act")
        pt_dve = sem("pt_dve")
        av_mm = sem("av_mm")
        rwide_done = sem("rwide_done")
        rt_mm = sem("rt_mm")
        rt_cp = sem("rt_cp")
        attn_done = sem("attn_done")
        y_mm = sem("y_mm")
        x2_done = sem("x2_done")
        ffn_mm = sem("ffn_mm")
        sig_done = sem("sig_done")
        hact_done = sem("hact_done")
        down_mm = sem("down_mm")
        fin_done = sem("fin_done")

        block = ctx.enter_context(nc.Block())
        PRE_STEPS, BATCH_STEPS, TAIL_STEPS = 3, 151, 22
        FIRST_STEPS = 2
        NX = 3
        AV_CUT = (KT + 1) // 2

        def batches(eng, body, tail):
            body(0, False)
            with eng.Fori(1, B) as b:
                body(b, True)
            tail(B - 1)

        @block.sync
        def _(sp):
            def load(s, dst, src):
                sp.dma_start(dst, src).then_inc(s, 16)

            def load_x(b):
                sp.dma_start(x_in[:, :, :], x[b].rearrange("(t p) d -> p t d", p=P)).then_inc(x_got, 16)

            def load_ctx(b):
                sp.dma_start(ctx_raw[:, 0:SK], ctx_t[b]).then_inc(ctx_got, 16)

            load_x(0)
            load(w_self, st_pq, pq_t)
            load(w_self, st_pk, pk_t)
            load(w_cross, st_wq, wq_t)
            load(w_cross, st_wk, wk_t)
            load(w_cross, w_wv, wv)
            load_ctx(0)
            rest = [
                (w_pv[:, :], pv), (w_po[:, :, :], po.rearrange("(c p) d -> p c d", p=P)),
                (w_wo[:, :, :], wo.rearrange("(c p) d -> p c d", p=P)),
                (bv_c[:, :], bv), (bo_in[:, :], bo.partition_broadcast(P)),
                (gamma_all[:, :], gamma.partition_broadcast(P)), (beta_all[:, :], beta.partition_broadcast(P)),
                (gate_int, w_gate_t), (up_int, w_up_t), (down_int, w_down_t.rearrange("(c p) d -> p c d", p=P)),
            ]
            assert len(rest) == N_REST
            for dst, src in rest:
                load(w_in, dst, src)
            for dst, src in ((wide_wq, wq), (wide_wk, wk), (wide_bq, bq.partition_broadcast(P)),
                             (wide_bk, bk.partition_broadcast(P))):
                load(w_bias, dst, src)
            with sp.Fori(1, B) as b:
                sp.wait_ge(x1_done, b)
                load_x(b)
                sp.wait_ge(ctxlo_done, b)
                load_ctx(b)

        @block.gpsimd
        def _(pool):
            pool.memset(ident[:, :], 0.0).then_inc(consts, 1)
            pool.memset(mask_b[:, :], 0.0).then_inc(consts, 1)
            pool.memset(nhalf[:, :], -0.5)
            pool.memset(ctx_raw[:, SK:SKP], 0.0)
            pool.wait_ge(consts, 2)
            pool.affine_select(out=ident[:, :], in_=ident[:, :], compare_op=ALU.not_equal, fill=1.0, base=0,
                               pattern=[[-1, P]], channel_multiplier=1).then_inc(consts, 1)
            pool.affine_select(out=mask_b[:, :], in_=mask_b[:, :], compare_op=ALU.is_ge, fill=MASKED, base=P,
                               pattern=[[-1, SQ]], channel_multiplier=1).then_inc(consts, 1)
            pool.wait_ge(consts, 4)
            pool.tensor_copy(ident_b[:, :], ident[:, :]).then_inc(consts, 1)
            pool.wait_ge(var_done, 1)
            pool.tensor_tensor(rstd[:, :], var[:, :], nhalf[:, :], ALU.pow).then_inc(rstd_done, 1)
            pool.wait_ge(w_bias, 64)
            pool.tensor_tensor(wide_wk, wide_wk, wide_bq, ALU.mult).then_inc(bias_mul, 1)
            pool.tensor_tensor(wide_wq, wide_wq, wide_bk, ALU.mult).then_inc(bias_mul, 1)
            pool.wait_ge(bias_mul, 2)
            pool.tensor_tensor(wide_bq, wide_bq, wide_bk, ALU.mult).then_inc(bias_mul, 1)
            with pool.Fori(1, 4 * B) as k:
                pool.wait_ge(var_done, k + 1)
                pool.tensor_tensor(rstd[:, :], var[:, :], nhalf[:, :], ALU.pow).then_inc(rstd_done, 1)

        @block.tensor
        def _(pe):
            pe.wait_ge(consts, 5)
            for g in range(8):
                pe.wait_ge(w_self if g < 4 else w_cross, 32 if g < 4 else 48)
                wa, wb = (st_pq, st_pk) if g < 4 else (st_wq, st_wk)
                for j in range(4):
                    h = 4 * (g % 4) + j
                    if g >= 4 and j == 0:
                        pe.wait_ge(fold_cp, g - 3)
                    mm = pe.matmul(ps_s[:, g % 4, j * D:(j + 1) * D], wa[:, h, :], wb[:, h, :], start=True, stop=True)
                mm.then_inc(fold_mm, 1)
            pe.wait_ge(prep, 2)
            pe.wait_ge(w_in, 16 * N_REST)
            for c in range(NC):
                mm = pe.matmul(ps_m[:, 0:D], bv_wide[:, c, :], w_wo[:, c, :], start=(c == 0), stop=(c == NC - 1))
            mm.then_inc(fold_mm, 1)
            pe.wait_ge(fold_cp, 9)
            pe.wait_ge(wvhi_done, 1)

            def transpose_rows(k, b):
                pe.wait_ge(xn_done[k], b + 1)
                for t in range(QT):
                    mm = pe.transpose(ps_m[:, t * P:(t + 1) * P], xn[k][:, t, :], ident[:, :])
                mm.then_inc(xt_mm[k], 1)

            def project_out(b):
                pe.wait_ge(attn_done, b * NJ + NJ)
                for t in range(QT):
                    for c in range(NP):
                        mm = pe.matmul(ps_o[:, t * P:(t + 1) * P], attn_t[:, c, t * P:(t + 1) * P], w_wo[:, c, :],
                                       start=(c == 0), stop=(c == NP - 1))
                mm.then_inc(y_mm, 1)

            def gate_up(b, c):
                bank = ps_h[c % 2]
                if c == 0:
                    pe.wait_ge(xt_cp[2], b + 1)
                if c >= 2:
                    pe.wait_ge(hact_done, b * HT + (c - 1))
                pe.matmul(bank[:, 0:SQ], gate_w[:, c * P:(c + 1) * P], xt[2][:, :], start=True, stop=True)
                pe.matmul(bank[:, SQ:2 * SQ], up_w[:, c * P:(c + 1) * P], xt[2][:, :], start=True,
                          stop=True).then_inc(ffn_mm, 1)

            def down(b):
                pe.wait_ge(hact_done, b * HT + HT)
                for t in range(QT):
                    for c in range(HT):
                        mm = pe.matmul(ps_o[:, t * P:(t + 1) * P], h_act[:, c, t * P:(t + 1) * P], down_w[:, c, :],
                                       start=(c == 0), stop=(c == HT - 1))
                mm.then_inc(down_mm, 1)

            def tail(b):
                project_out(b)
                transpose_rows(2, b)
                for c in range(HT):
                    gate_up(b, c)
                down(b)

            def body(b, follows):
                v_next = [0]

                def values(n):
                    for k in range(v_next[0], v_next[0] + n):
                        i, half = k // 2, k % 2
                        rows = P if i < KT - 1 else KL
                        keys, cols = slice(i * P, i * P + rows), slice(half * 512, half * 512 + 512)
                        if k == 0:
                            pe.wait_ge(ctxhi_done, b + 1)
                            pe.wait_ge(ctxlo_done, b + 1)
                        if k >= 2:
                            pe.wait_ge(v_cp, b * NV + (k - 1))
                        dst = ps_s[0:rows, 2 + k % 2, :]
                        pe.matmul(dst, ctx_hi[:, keys], wv_hi[:, cols], start=True, stop=False)
                        pe.matmul(dst, ctx_hi[:, keys], wv_lo[:, cols], start=False, stop=False)
                        pe.matmul(dst, ctx_lo[:, keys], wv_hi[:, cols], start=False, stop=True).then_inc(v_mm, 1)
                    v_next[0] += n

                def self_q(p):
                    if p >= 2:
                        pe.wait_ge(qs_cp, b * NP + (p - 1))
                    for a in range(2):
                        mm = pe.matmul(ps_t[p % 2][:, a * SQ:(a + 1) * SQ], qk_self[:, 2 * p + a, :], xt[0][:, :],
                                       start=True, stop=True)
                    mm.then_inc(qs_mm, 1)

                if follows:
                    project_out(b - 1)
                transpose_rows(0, b)
                pe.wait_ge(xt_cp[0], b + 1)
                self_q(0)
                values(1)
                for h in range(H):
                    if h % 2 == 0 and h // 2 + 1 < NP:
                        self_q(h // 2 + 1)
                    if h > 0:
                        values(1)
                    pe.wait_ge(qs_cp, b * NP + (h // 2 + 1))
                    if h >= 2:
                        pe.wait_ge(es_done, b * H + (h - 1))
                    q = qs[:, (h // 2) % 2, (h % 2) * SQ:(h % 2 + 1) * SQ]
                    bank = ps_s[:, h % 2, :]
                    pe.matmul(bank[:, 0:P], q[:, 0:P], xt[0][:, 0:P], start=True, stop=False)
                    pe.matmul(bank[:, 0:P], ident_b[:, :], mask_b[:, P:SQ], start=False, stop=True)
                    pe.matmul(bank[:, P:P + SQ], q[:, P:SQ], xt[0][:, :], start=True, stop=False)
                    pe.matmul(bank[:, P:P + SQ], ident_b[:, :], mask_b[:, :], start=False,
                              stop=True).then_inc(logit_mm, 1)
                    if follows and h == 4:
                        transpose_rows(2, b - 1)
                    if follows and h == 5:
                        gate_up(b - 1, 0)
                        gate_up(b - 1, 1)
                    if follows and h == 9:
                        gate_up(b - 1, 2)

                def self_values(t):
                    if t == 0:
                        pe.wait_ge(qs_cp, b * NP + NP)
                    else:
                        pe.wait_ge(os_done, b * QT + t)
                    for n in range(2):
                        mm = pe.matmul(ps_t[n][:, :], xt[0][:, t * P:(t + 1) * P], w_pv[:, n * 512:(n + 1) * 512],
                                       start=True, stop=True)
                    mm.then_inc(vs_mm, 1)

                def turn_self(t):
                    pe.wait_ge(os_done, b * QT + (t + 1))
                    if t == 0:
                        pe.wait_ge(es_done, b * H + H)
                    for c in range(NC):
                        mm = pe.transpose(ps_s[:, c // 4, (c % 4) * P:(c % 4 + 1) * P],
                                          o_self[:, t, c * P:(c + 1) * P], ident[:, :])
                    mm.then_inc(ot_mm, 1)

                def project_self(t):
                    pe.wait_ge(ot_cp, b * QT + (t + 1))
                    if t == 0 and follows:
                        pe.wait_ge(fin_done, b)
                    for c in range(NC):
                        mm = pe.matmul(ps_o[:, t * P:(t + 1) * P], o_self_t[:, c, :], w_po[:, c, :],
                                       start=(c == 0), stop=(c == NC - 1))
                    mm.then_inc(ys_mm, 1)

                self_values(0)
                values(2)
                if follows:
                    down(b - 1)
                turn_self(0)
                self_values(1)
                values(2)
                project_self(0)
                turn_self(1)
                values(2)
                project_self(1)
                values(2)

                transpose_rows(1, b)
                values(1)
                pe.wait_ge(xt_cp[1], b + 1)
                pe.wait_ge(bias_done, 1)
                for t in range(QT):
                    mm = pe.matmul(ps_o[:, t * H:(t + 1) * H], xt[1][:, t * P:(t + 1) * P], ub[:, :],
                                   start=True, stop=True)
                mm.then_inc(t_mm, 1)

                def cross_q(p):
                    for a in range(2):
                        mm = pe.matmul(ps_m[:, a * SQ:(a + 1) * SQ], qk_cross[:, 2 * p + a, :], xt[1][:, :],
                                       start=True, stop=True)
                    mm.then_inc(q_mm, 1)

                def scores(u):
                    p, t, a = u // 4, u // 2 % 2, u % 2
                    at = a * SQ + t * P
                    hi, lo = q_hi[:, p % 2, at:at + P], q_lo[:, p % 2, at:at + P]
                    pe.wait_ge(qhi_done, b * NP + (p + 1))
                    pe.wait_ge(qlo_done, b * NP + (p + 1))
                    if u == 0:
                        pe.wait_ge(v_cp, b * NV + NV)
                    for c in range(CH):
                        if u > 0 and c != 1:
                            pe.wait_ge(exp_done, b * NU * NX + (NX * (u - 1) + max(c, 1)))
                        n = CW if c < CH - 1 else SKP - (CH - 1) * CW
                        keys, dst = slice(c * CW, c * CW + n), ps_s[:, c, 0:n]
                        pe.matmul(dst, hi, ctx_hi[:, keys], start=True, stop=False)
                        pe.matmul(dst, hi, ctx_lo[:, keys], start=False, stop=False)
                        pe.matmul(dst, lo, ctx_hi[:, keys], start=False, stop=True).then_inc(s_mm, 1)

                def transposes(u, groups):
                    for g in groups:
                        if g < NX:
                            pe.wait_ge(exp_done, b * NU * NX + (NX * u + g + 1))
                        if u > 0 or g >= 2:
                            pe.wait_ge(pt_act if g % 2 == 0 else pt_dve, b * NU * 2 + (2 * u + g // 2))
                        for i in range(4 * g, min(4 * g + 4, KT)):
                            n = P if i < KT - 1 else KL
                            mm = pe.transpose(ps_t[g % 2][0:n, (i % 4) * P:(i % 4 + 1) * P],
                                              probs[:, u % 2, i * P:i * P + n], ident[:, :])
                        mm.then_inc(pt_mm, 1)

                def weigh(j, part):
                    p = j // QT
                    if part == 0:
                        pe.wait_ge(pt_act, b * NU * 2 + 4 * (j + 1))
                        pe.wait_ge(pt_dve, b * NU * 2 + 4 * (j + 1))
                        if j == 0:
                            pe.wait_ge(t_done, b + 1)
                        else:
                            pe.wait_ge(attn_done, b * NJ + j)
                    for i in range(0, AV_CUT) if part == 0 else range(AV_CUT, KT):
                        rows = P if i < KT - 1 else KL
                        for a in range(2):
                            at = (2 * p + a) * DK
                            mm = pe.matmul(ps_o[a * DK:(a + 1) * DK, 0:P], vals[0:rows, i, at:at + DK],
                                           probs_t[0:rows, j % 2, a, i, :], start=(i == 0), stop=(i == KT - 1),
                                           skip_group_check=True)
                    if part == 1:
                        mm.then_inc(av_mm, 1)

                def turn_weights(j):
                    pe.wait_ge(rwide_done, b * NJ + (j + 1))
                    if j > 0:
                        pe.wait_ge(rt_cp, b * NJ + j)
                    pe.wait_ge(qlo_done, b * NP + min((2 * j + 2) // 4 + 1, NP))
                    pe.transpose(ps_m[:, 0:P], rwide[:, :, :].rearrange("p a k -> p (a k)"),
                                 ident[:, :]).then_inc(rt_mm, 1)

                cross_q(0)
                values(1)
                scores(0)
                for u in range(NU):
                    if u + 1 < NU:
                        scores(u + 1)
                    transposes(u, (0, 1))
                    if u >= 2:
                        weigh(u // 2 - 1, u % 2)
                    transposes(u, range(2, TG))
                    if u >= 2:
                        if u % 2 == 0:
                            turn_weights(u // 2 - 1)
                    if u % 4 == 1 and u // 4 + 1 < NP:
                        if u > 4:
                            pe.wait_ge(rt_cp, b * NJ + (u // 2))
                        cross_q(u // 4 + 1)
                weigh(NJ - 1, 0)
                turn_weights(NJ - 1)
                weigh(NJ - 1, 1)

            batches(pe, body, tail)

        @block.scalar
        def _(act):
            act.wait_ge(w_cross, 48)
            act.activation(wv_hi[:, :], w_wv, ACT.Copy).then_inc(wvhi_done, 1)

            def copy_rows(k, b):
                act.wait_ge(xt_mm[k], b + 1)
                act.activation(xt[k][:, :], ps_m[:, 0:SQ], ACT.Copy).then_inc(xt_cp[k], 1)

            def gate_exp(b, c):
                act.wait_ge(ffn_mm, b * HT + (c + 1))
                act.activation(h_e[:, c, :], ps_h[c % 2][:, 0:SQ], ACT.Exp, scale=-1.0).then_inc(sig_done, 1)

            def store(b):
                act.wait_ge(fin_done, b + 1)
                act.dma_start(out[b].rearrange("(t p) d -> p t d", p=P), fin[:, :, :]).then_inc(out_put, 16)

            def tail(b):
                copy_rows(2, b)
                for c in range(HT):
                    gate_exp(b, c)
                store(b)
                act.wait_ge(out_put, 16 * (b + 1))

            def body(b, follows):
                v_next = [0]

                def values(n):
                    for k in range(v_next[0], v_next[0] + n):
                        rows = P if k // 2 < KT - 1 else KL
                        act.wait_ge(v_mm, b * NV + (k + 1))
                        act.activation(vals[0:rows, k // 2, (k % 2) * 512:(k % 2 + 1) * 512],
                                       ps_s[0:rows, 2 + k % 2, :], ACT.Copy).then_inc(v_cp, 1)
                    v_next[0] += n

                def self_q(p):
                    act.wait_ge(qs_mm, b * NP + (p + 1))
                    if p >= 2:
                        act.wait_ge(logit_mm, b * H + 2 * (p - 1))
                    act.activation(qs[:, p % 2, :], ps_t[p % 2][:, :], ACT.Copy).then_inc(qs_cp, 1)

                act.wait_ge(ctx_got, b * 16 + 16)
                act.wait_ge(consts, 5)
                if follows:
                    act.wait_ge(s_mm, b * NU * CH)
                act.activation(ctx_hi[:, :], ctx_raw[:, :], ACT.Copy).then_inc(ctxhi_done, 1)
                copy_rows(0, b)
                self_q(0)
                values(1)
                for h in range(H):
                    if h % 2 == 0 and h // 2 + 1 < NP:
                        self_q(h // 2 + 1)
                    if h > 0:
                        values(1)
                    act.wait_ge(nmax_done, b * H + (h + 1))
                    if h >= 2:
                        act.wait_ge(diag_done, b * H + (h - 1))
                    for t in range(QT):
                        lo, n = t * P, (t + 1) * P
                        ins = act.activation(es[:, h % 2, lo:lo + n], ps_s[:, h % 2, lo:lo + n], ACT.Exp,
                                             bias=nmx8[:, h, t:t + 1], scale=SHARP, accum_out=sums_s[:, t, h:h + 1])
                    ins.then_inc(es_done, 1)
                    if follows and h == 4:
                        copy_rows(2, b - 1)
                    if follows and h == 5:
                        gate_exp(b - 1, 0)
                        gate_exp(b - 1, 1)
                    if follows and h == 9:
                        gate_exp(b - 1, 2)

                def copy_self(t):
                    act.wait_ge(ot_mm, b * QT + (t + 1))
                    if t > 0:
                        act.wait_ge(ys_mm, b * QT + t)
                    act.activation(o_self_t[:, :, :], ps_s[:, 0:2, :].rearrange("p b (c n) -> p (b c) n", n=P),
                                   ACT.Copy).then_inc(ot_cp, 1)

                values(2)
                copy_self(0)
                values(2)
                copy_self(1)
                values(2)
                if follows:
                    store(b - 1)
                values(2)
                copy_rows(1, b)
                values(1)

                def cross_q_hi(p):
                    act.wait_ge(q_mm, b * NP + (p + 1))
                    for a in range(2):
                        ins = act.activation(q_hi[:, p % 2, a * SQ:(a + 1) * SQ], ps_m[:, a * SQ:(a + 1) * SQ],
                                             ACT.Identity, bias=qbias[:, 2 * p + a:2 * p + a + 1])
                    ins.then_inc(qhi_done, 1)

                def exps(u):
                    act.wait_ge(ebias_done, b * NU + (u + 1))
                    if u >= 2:
                        act.wait_ge(pt_mm, b * NU * TG + TG * (u - 1))
                    for k in range(NX):
                        c, n = (0, 2) if k == 0 else (k + 1, 1)
                        w = CW if c < CH - 1 else CL
                        act.activation(probs[:, u % 2, c * CW:c * CW + n * w].rearrange("p (c k) -> p c k", c=n),
                                       ps_s[:, c:c + n, 0:w], ACT.Exp, bias=ebias[:, u % 2:u % 2 + 1], scale=TEMP,
                                       accum_out=sums[:, u % 8, k:k + 1]).then_inc(exp_done, 1)

                def copy_group(u, g):
                    j, a = u // 2, u % 2
                    act.wait_ge(pt_mm, b * NU * TG + (TG * u + g + 1))
                    if g == 0 and j >= 2:
                        act.wait_ge(av_mm, b * NJ + (j - 1))
                    n = min(4, KT - 4 * g)
                    act.activation(probs_t[:, j % 2, a, 4 * g:4 * g + n, :],
                                   ps_t[0][:, 0:n * P].rearrange("p (i q) -> p i q", q=P),
                                   ACT.Copy).then_inc(pt_act, 1)

                def copy_weights(j):
                    act.wait_ge(rt_mm, b * NJ + (j + 1))
                    if j > 0:
                        act.wait_ge(attn_done, b * NJ + j)
                    act.activation(rt[:, :], ps_m[:, 0:P], ACT.Copy).then_inc(rt_cp, 1)

                cross_q_hi(0)
                values(1)
                exps(0)
                for u in range(NU):
                    copy_group(u, 0)
                    if u + 1 < NU:
                        exps(u + 1)
                    copy_group(u, 2)
                    if u % 2 == 0 and u > 0:
                        copy_weights(u // 2 - 1)
                    if u % 4 == 1 and u // 4 + 1 < NP:
                        cross_q_hi(u // 4 + 1)
                copy_weights(NJ - 1)
                if follows:
                    act.wait_ge(out_put, b * 16)

            batches(act, body, tail)

        @block.vector
        def _(dve):
            steps, base = [0], [0]

            def then(ins):
                steps[0] += 1
                ins.then_inc(dve_step, 1)
                dve.wait_ge(dve_step, base[0] + steps[0])

            def normalise(k, src, dst):
                for t in range(QT):
                    ins = dve.bn_stats(stats[:, t, :], src[:, t, :])
                then(ins)
                dve.memset(spare[:, :], 0.0)
                for t in range(QT):
                    ins = dve.bn_aggr(mv[:, t, :], stats[:, t, :])
                then(ins)
                dve.tensor_scalar(var[:, :], mv[:, :, 1], EPS, None, ALU.add).then_inc(var_done, 1)
                dve.wait_ge(rstd_done, k + 1)
                for t in range(QT):
                    ins = dve.tensor_scalar(dst[:, t, :], src[:, t, :], mv[:, t, 0:1], rstd[:, t:t + 1],
                                            ALU.subtract, ALU.mult)
                return ins

            dve.wait_ge(x_got, 16)
            normalise(0, x_in, xn[0]).then_inc(xn_done[0], 1)
            for g in range(4):
                dve.wait_ge(fold_mm, g + 1)
                dve.tensor_copy(qk_self[:, 4 * g:4 * g + 4, :],
                                ps_s[:, g, :].rearrange("p (h d) -> p h d", h=4)).then_inc(fold_cp, 1)
            dve.wait_ge(wvhi_done, 1)
            dve.tensor_tensor(wv_lo[:, :], w_wv, wv_hi[:, :].bitcast(F32), ALU.subtract).then_inc(prep, 1)
            for g in range(4):
                dve.wait_ge(fold_mm, g + 5)
                dve.tensor_copy(qk_cross[:, 4 * g:4 * g + 4, :],
                                ps_s[:, g, :].rearrange("p (h d) -> p h d", h=4)).then_inc(fold_cp, 1)
            dve.wait_ge(w_in, 16 * N_REST)
            dve.tensor_copy(bv_wide, bv_c[:, :].unsqueeze(2).broadcast_to([P, NC, P])).then_inc(prep, 1)
            dve.tensor_scalar(gate_w[:, :], gate_int, 1.0 / 127.0, None, ALU.mult)
            dve.tensor_scalar(up_w[:, :], up_int, 1.0 / 127.0, None, ALU.mult)
            then(dve.tensor_scalar(down_w[:, :, :], down_int, 1.0 / 127.0, None, ALU.mult))
            dve.wait_ge(fold_mm, 9)
            dve.tensor_tensor(bo_all[:, :], ps_m[:, 0:D], bo_in[:, :], ALU.add).then_inc(fold_cp, 1)
            assert steps[0] == PRE_STEPS

            def tail_rows(b, k):
                dve.wait_ge(y_mm, b + 1)
                for t in range(QT):
                    ins = dve.tensor_tensor(y[:, t, :], ps_o[:, t * P:(t + 1) * P], bo_all[:, :], ALU.add)
                then(ins)
                then(dve.tensor_tensor(y[:, :, :], y[:, :, :], xn[1][:, :, :], ALU.add))
                then(normalise(k, y, y))
                for t in range(QT):
                    ins = dve.tensor_tensor(y[:, t, :], y[:, t, :], gamma_all[:, :], ALU.mult)
                then(ins)
                for t in range(QT):
                    ins = dve.tensor_tensor(y[:, t, :], y[:, t, :], beta_all[:, :], ALU.add)
                then(ins)
                then(dve.tensor_tensor(x2[:, :, :], x1[:, :, :], y[:, :, :], ALU.add))
                normalise(k + 1, x2, xn[2]).then_inc(xn_done[2], 1)

            def tail_hidden(b, c, parts=(0, 1, 2)):
                if 0 in parts:
                    dve.wait_ge(sig_done, b * HT + (c + 1))
                    then(dve.tensor_scalar(h_e[:, c, :], h_e[:, c, :], 1.0, None, ALU.add))
                    then(dve.reciprocal(h_e[:, c, 0:P], h_e[:, c, 0:P]))
                if 1 in parts:
                    then(dve.reciprocal(h_e[:, c, P:SQ], h_e[:, c, P:SQ]))
                if 2 in parts:
                    bank = ps_h[c % 2]
                    then(dve.tensor_tensor(h_e[:, c, :], bank[:, 0:SQ], h_e[:, c, :], ALU.mult))
                    dve.tensor_tensor(h_act[:, c, :], bank[:, SQ:2 * SQ], h_e[:, c, :],
                                      ALU.mult).then_inc(hact_done, 1)

            def tail_out(b):
                dve.wait_ge(down_mm, b + 1)
                dve.tensor_tensor(fin[:, :, :], ps_o[:, 0:SQ].rearrange("p (t d) -> p t d", d=D), x2[:, :, :],
                                  ALU.add).then_inc(fin_done, 1)

            def tail(b):
                steps[0] = BATCH_STEPS
                base[0] = b * (BATCH_STEPS + TAIL_STEPS) + (PRE_STEPS - FIRST_STEPS)
                tail_rows(b, 4 * b + 2)
                for c in range(HT):
                    tail_hidden(b, c)
                dve.wait_ge(out_put, b * 16)
                tail_out(b)

            def body(b, follows):
                if follows:
                    steps[0] = 0
                    base[0] = b * (BATCH_STEPS + TAIL_STEPS) + (PRE_STEPS - FIRST_STEPS - TAIL_STEPS)
                else:
                    steps[0] = FIRST_STEPS
                    base[0] = PRE_STEPS - FIRST_STEPS
                if follows:
                    dve.wait_ge(x_got, b * 16 + 16)
                    normalise(4 * b - 2, x_in, xn[0]).then_inc(xn_done[0], 1)
                dve.wait_ge(ctxhi_done, b + 1)
                dve.tensor_tensor(ctx_lo[:, :], ctx_raw[:, :], ctx_hi[:, :].bitcast(F32),
                                  ALU.subtract).then_inc(ctxlo_done, 1)
                if follows:
                    tail_rows(b - 1, 4 * b - 1)

                def diagonal(h):
                    dve.wait_ge(es_done, b * H + (h + 1))
                    for t in range(QT):
                        ins = dve.scalar_tensor_tensor(out=junk[:, h % 2, t, :],
                                                       in0=es[:, h % 2, 2 * t * P:(2 * t + 1) * P],
                                                       scalar=1.0, in1=ident[:, :], op0=ALU.mult, op1=ALU.mult,
                                                       accum_out=diag_s[:, t, h:h + 1])
                    ins.then_inc(diag_done, 1)

                for h in range(H):
                    dve.wait_ge(logit_mm, b * H + (h + 1))
                    for t in range(QT):
                        lo, n = t * P, (t + 1) * P
                        ins = dve.tensor_reduce(nmx[:, h, t:t + 1], ps_s[:, h % 2, lo:lo + n], AX.X, ALU.max,
                                                negate=True)
                    then(ins)
                    dve.tensor_scalar(nmx8[:, h, :], nmx[:, h, :], SHARP, None, ALU.mult).then_inc(nmax_done, 1)
                    if h > 0:
                        diagonal(h - 1)
                    if follows and 6 <= h < 6 + 3 * HT:
                        tail_hidden(b - 1, (h - 6) // 3, ((h - 6) % 3,))
                diagonal(H - 1)
                then(dve.reciprocal(rsum_s[:, :, :], sums_s[:, :, :]))
                dve.wait_ge(diag_done, b * H + H)
                then(dve.tensor_tensor(wdiag[:, :, :], diag_s[:, :, :], rsum_s[:, :, :], ALU.mult))
                for t in range(QT):
                    dve.wait_ge(vs_mm, b * QT + (t + 1))
                    for n in range(2):
                        w = wdiag[:, t, 8 * n:8 * n + 8].unsqueeze(2).broadcast_to([P, 8, DK])
                        ins = dve.tensor_tensor(o_self[:, t, n * 512:(n + 1) * 512].rearrange("p (h k) -> p h k", k=DK),
                                                ps_t[n][:, :].rearrange("p (h k) -> p h k", k=DK), w, ALU.mult)
                    ins.then_inc(os_done, 1)
                    if follows and t == 0:
                        tail_out(b - 1)
                    if not follows and t == 0:
                        for k, (dst, src) in enumerate(((qbias, wide_wk), (ub, wide_wq), (t0, wide_bq))):
                            dve.wait_ge(bias_mul, k + 1)
                            ins = dve.tensor_reduce(dst[:, :], src.rearrange("p (h k) -> p h k", k=DK), AX.X, ALU.add)
                        ins.then_inc(bias_done, 1)
                dve.wait_ge(ys_mm, b * QT + QT)
                ins = dve.tensor_tensor(x1[:, :, :], ps_o[:, 0:SQ].rearrange("p (t d) -> p t d", d=D), x_in[:, :, :],
                                        ALU.add)
                ins.then_inc(x1_done, 1)
                dve.wait_ge(x1_done, b + 1)
                normalise(4 * b + 1, x1, xn[1]).then_inc(xn_done[1], 1)

                dve.wait_ge(t_mm, b + 1)
                for t in range(QT):
                    ins = dve.tensor_tensor(tterm[:, t, :], ps_o[:, t * H:(t + 1) * H], t0[:, :], ALU.add)
                then(ins)
                dve.tensor_scalar(tterm8[:, :, :], tterm[:, :, :], TEMP, None, ALU.mult).then_inc(t_done, 1)
                dve.wait_ge(t_done, b + 1)

                def cross_q_lo(p):
                    dve.wait_ge(qhi_done, b * NP + (p + 1))
                    for a in range(2):
                        cols = slice(a * SQ, (a + 1) * SQ)
                        ins = dve.scalar_tensor_tensor(out=q_lo[:, p % 2, cols], in0=ps_m[:, cols],
                                                       scalar=qbias[:, 2 * p + a:2 * p + a + 1],
                                                       in1=q_hi[:, p % 2, cols].bitcast(F32),
                                                       op0=ALU.add, op1=ALU.subtract)
                    ins.then_inc(qlo_done, 1)

                def maxima(u):
                    h, t = 2 * (u // 4) + u % 2, u // 2 % 2
                    for c in range(CH):
                        dve.wait_ge(s_mm, b * NU * CH + (CH * u + c + 1))
                        ins = dve.tensor_reduce(mx4[:, c:c + 1], ps_s[:, c, 0:CW if c < CH - 1 else CL], AX.X, ALU.max)
                        if c == CH - 2:
                            then(ins)
                            ins = dve.tensor_reduce(mx3[:, :], mx4[:, 0:CH - 1], AX.X, ALU.max)
                    then(ins)
                    then(dve.scalar_tensor_tensor(out=nb[:, :], in0=mx4[:, CH - 1:CH], scalar=mx3[:, :],
                                                  in1=tterm[:, t, h:h + 1], op0=ALU.max, op1=ALU.add))
                    if u >= 2:
                        dve.wait_ge(exp_done, b * NU * NX + NX * (u - 1))
                    dve.scalar_tensor_tensor(out=ebias[:, u % 2:u % 2 + 1], in0=nb[:, :], scalar=-TEMP,
                                             in1=tterm8[:, t, h:h + 1], op0=ALU.mult,
                                             op1=ALU.add).then_inc(ebias_done, 1)

                def copy_group(u, g):
                    j, a = u // 2, u % 2
                    dve.wait_ge(pt_mm, b * NU * TG + (TG * u + g + 1))
                    if g == 1 and j >= 2:
                        dve.wait_ge(av_mm, b * NJ + (j - 1))
                    n = min(4, KT - 4 * g)
                    rows = P if g < TG - 1 else KL
                    dve.tensor_copy(probs_t[0:rows, j % 2, a, 4 * g:4 * g + n, :],
                                    ps_t[1][0:rows, 0:n * P].rearrange("p (i q) -> p i q", q=P)).then_inc(pt_dve, 1)

                def weights_wide(j):
                    s0 = 2 * (j % 4)
                    dve.wait_ge(exp_done, b * NU * NX + NX * (2 * j + 2))
                    then(dve.tensor_reduce(sum1[:, :], sums[:, s0:s0 + 2, :], AX.X, ALU.add))
                    then(dve.reciprocal(rsum[:, :], sum1[:, :]))
                    if j > 0:
                        dve.wait_ge(rt_mm, b * NJ + j)
                    dve.tensor_copy(rwide[:, :, :], rsum[:, :].unsqueeze(2).broadcast_to([P, 2, DK])).then_inc(rwide_done, 1)

                def normal_out(j):
                    p, t = j // QT, j % QT
                    dve.wait_ge(rt_cp, b * NJ + (j + 1))
                    dve.wait_ge(av_mm, b * NJ + (j + 1))
                    dve.tensor_tensor(attn_t[:, p, t * P:(t + 1) * P], ps_o[:, 0:P], rt[:, :],
                                      ALU.mult).then_inc(attn_done, 1)

                cross_q_lo(0)
                maxima(0)
                for u in range(NU):
                    if u % 2 == 0 and u >= 4:
                        normal_out(u // 2 - 2)
                    if u + 1 < NU:
                        maxima(u + 1)
                    copy_group(u, 1)
                    copy_group(u, 3)
                    if u % 2 == 1:
                        weights_wide(u // 2)
                    if u % 4 == 1 and u // 4 + 1 < NP:
                        cross_q_lo(u // 4 + 1)
                normal_out(NJ - 2)
                normal_out(NJ - 1)
                assert steps[0] == BATCH_STEPS + (TAIL_STEPS if follows else 0)

            batches(dve, body, tail)


def kernel(**inputs):
    import numpy as np
    import concourse.bacc as bacc
    from concourse.bass_utils import run_bass_kernel_spmd

    a = {k: np.asarray(v) for k, v in inputs.items()}

    def heads_last(w):
        return w.transpose(2, 0, 1)

    def by_head(w):
        return w.reshape(w.shape[0], -1, 64).transpose(2, 1, 0)

    laid = {
        "x": a["x"],
        "ctx_t": a["ctx_1024"].transpose(0, 2, 1),
        "pq_t": heads_last(a["L0_attn_P_q"]),
        "pk_t": heads_last(a["L0_attn_P_k"]),
        "pv": a["L0_attn_P_v"].transpose(1, 0, 2).reshape(128, -1),
        "po": a["L0_attn_P_o"].transpose(0, 2, 1).reshape(-1, 128),
        "wq_t": by_head(a["L0_xattn_Wq"]),
        "wk_t": by_head(a["L0_xattn_Wk"]),
        "wq": a["L0_xattn_Wq"],
        "wk": a["L0_xattn_Wk"],
        "bq": a["L0_xattn_bq"],
        "bk": a["L0_xattn_bk"],
        "wv": a["L0_xattn_Wv"],
        "bv": a["L0_xattn_bv"].reshape(-1, 128).T,
        "wo": a["L0_xattn_Wo"],
        "bo": a["L0_xattn_bo"],
        "gamma": a["L0_xattn_ln_gamma"],
        "beta": a["L0_xattn_ln_beta"],
        "w_gate_t": a["L0_ffn_w_gate"].T,
        "w_up_t": a["L0_ffn_w_up"].T,
        "w_down_t": a["L0_ffn_w_down"].T,
    }
    nc = bacc.Bacc("TRN2", target_bir_lowering=False, num_devices=1)
    arrays, args = {}, []
    for name, v in laid.items():
        v = np.ascontiguousarray(v)
        arrays[f"in_{name}"] = v
        args.append(nc.dram_tensor(f"in_{name}", v.shape, mybir.dt.from_np(v.dtype), kind="ExternalInput").ap())
    out = nc.dram_tensor("out_x", a["x"].shape, F32, kind="ExternalOutput").ap()
    decoder_layer(nc, *args, out)
    r = run_bass_kernel_spmd(nc, [arrays], core_ids=[0])
    return r.results[0]["out_x"]
```

```python
from contextlib import ExitStack

import concourse.bass as bass
from concourse import mybir

ALU = mybir.AluOpType
ACT = mybir.ActivationFunctionType
AX = mybir.AxisListType
F32 = mybir.dt.float32
F32R = mybir.dt.float32r
BF16 = mybir.dt.bfloat16
I32 = mybir.dt.int32

EPS = 1e-5
MASKED = -1e30


def decoder_layer(nc, x, ctx_t, pq_t, pk_t, pv, po, wq_t, wk_t, wq, wk, bq, bk, wv, bv, wo, bo, gamma, beta,
                  w_gate_t, w_up_t, w_down_t, out):
    B, SQ, D = x.shape
    SK = ctx_t.shape[2]
    DK, H = pq_t.shape[0] // 2, pq_t.shape[1] * 2
    HV = wv.shape[1]
    P = 128
    QT = SQ // P
    NP = H // 2
    NC = HV // P
    KT = -(-SK // P)
    KL = SK - (KT - 1) * P
    CH = 4
    CW = SK // CH
    CL = SK - (CH - 1) * CW
    SKP = SK + SK % 2
    HID = w_gate_t.shape[1]
    HT = HID // P
    TEMP = 1.0 / float(DK) ** 0.5
    SHARP = float(DK) ** 0.5
    NU = H * QT
    NJ = NP * QT
    TG = -(-KT // 4)
    N_REST = 10
    NV = KT * 2

    with ExitStack() as ctx:
        def sb(name, shape, dt=F32):
            return ctx.enter_context(nc.sbuf_tensor(name, shape, dt))

        def pb(name, shape):
            return ctx.enter_context(nc.psum_tensor(name, shape, F32))

        def sem(name):
            return ctx.enter_context(nc.semaphore(name))

        w_pv = sb("w_pv", [P, HV])
        w_po = sb("w_po", [P, NC, D])
        w_wo = sb("w_wo", [P, NC, D])
        wv_hi = sb("wv_hi", [P, HV], F32R)
        wv_lo = sb("wv_lo", [P, HV], F32R)
        qk_self_hi, qk_self_lo = sb("qk_self_hi", [P, H, D], F32R), sb("qk_self_lo", [P, H, D], F32R)
        qk_cross_hi, qk_cross_lo = sb("qk_cross_hi", [P, H, D], F32R), sb("qk_cross_lo", [P, H, D], F32R)
        qbias = sb("qbias", [P, H])
        ub = sb("ub", [P, H])
        t0 = sb("t0", [P, H])
        bv_c = sb("bv_c", [P, NC])
        bo_in = sb("bo_in", [P, D])
        bo_all = sb("bo_all", [P, D])
        gamma_all = sb("gamma_all", [P, D])
        beta_all = sb("beta_all", [P, D])
        gate_w = sb("gate_w", [P, HID])
        up_w = sb("up_w", [P, HID])
        down_w = sb("down_w", [P, HT, D])
        ident = sb("ident", [P, P])
        ident_b = sb("ident_b", [P, P], BF16)
        mask_b = sb("mask_b", [P, P], BF16)
        nhalf = sb("nhalf", [P, QT])

        x_in = sb("x_in", [P, QT, D])
        x1 = sb("x1", [P, QT, D])
        x2 = sb("x2", [P, QT, D])
        xn = [sb(f"xn{k}", [P, QT, D]) for k in range(3)]
        xt = [sb(f"xt{k}", [P, SQ]) for k in range(3)]
        xt_hi = [sb(f"xt_hi{k}", [P, SQ], F32R) for k in range(2)]
        xt_lo = [sb(f"xt_lo{k}", [P, SQ], F32R) for k in range(2)]
        spare = sb("spare", [P, 1])
        stats = sb("stats", [P, QT, 6])
        mv = sb("mv", [P, QT, 2])
        var = sb("var", [P, QT])
        rstd = sb("rstd", [P, QT])
        ctx_raw = sb("ctx_raw", [P, SKP])
        ctx_hi = sb("ctx_hi", [P, SKP], F32R)
        ctx_lo = sb("ctx_lo", [P, SKP], F32R)
        vals = sb("vals", [P, KT, HV])
        nmx = sb("nmx", [P, H, QT])
        nmx8 = sb("nmx8", [P, H, QT])
        sums_s = sb("sums_s", [P, QT, H])
        diag_s = sb("diag_s", [P, QT, H])
        rsum_s = sb("rsum_s", [P, QT, H])
        wdiag = sb("wdiag", [P, QT, H])
        tterm = sb("tterm", [P, QT, H])
        tterm8 = sb("tterm8", [P, QT, H])
        q_hi = sb("q_hi", [P, 2, 2 * SQ], F32R)
        q_lo = sb("q_lo", [P, 2, 2 * SQ], F32R)
        mx4 = sb("mx4", [P, CH])
        mx3 = sb("mx3", [P, 1])
        nb = sb("nb", [P, 1])
        ebias = sb("ebias", [P, 2])
        probs = sb("probs", [P, 2, SK])
        probs_t = sb("probs_t", [P, 2, 2, KT, P])
        sums = sb("sums", [P, 8, 3])
        sum1 = sb("sum1", [P, 2])
        rsum = sb("rsum", [P, 2])
        rwide = sb("rwide", [P, 2, DK])
        rt = sb("rt", [P, P])
        attn_t = sb("attn_t", [P, NP, SQ])
        o_self = probs[:, :, 0:HV]
        rooms = [probs_t[:, j, :, :, :].rearrange("p a i q -> p (a i q)") for j in range(2)]
        qs = rooms[0][:, 0:4 * SQ].rearrange("p (s n) -> p s n", s=2)
        es = rooms[0][:, 4 * SQ:4 * SQ + 2 * (P + SQ)].rearrange("p (s n) -> p s n", s=2)
        junk = rooms[0][:, 7 * SQ:9 * SQ].rearrange("p (s t n) -> p s t n", s=2, t=QT)
        o_self_t = rooms[0][:, 9 * SQ:9 * SQ + HV].rearrange("p (c n) -> p c n", c=NC)
        h_e = rooms[1][:, 0:HT * SQ].rearrange("p (c n) -> p c n", c=HT)
        h_act = rooms[1][:, HT * SQ:2 * HT * SQ].rearrange("p (c n) -> p c n", c=HT)
        wide_wq, wide_wk, wide_bq = (rooms[1][:, i * HV:(i + 1) * HV] for i in range(3))
        wide_bk = attn_t[:, :, :].rearrange("p c n -> p (c n)")[:, 0:HV]
        y = sb("y", [P, QT, D])
        fin = sb("fin", [P, QT, D])

        stage = vals[:, :, :].rearrange("p k v -> p (k v)")
        st_pq, st_pk, st_wq, st_wk = (
            stage[:, i * NP * D:(i + 1) * NP * D].rearrange("p (h d) -> p h d", h=NP) for i in range(4))
        w_wv = stage[:, 4 * H * D:4 * H * D + HV]
        ints = stage[:, 4 * H * D + HV:4 * H * D + HV + 3 * HID].bitcast(I32)
        gate_int, up_int = ints[:, 0:HID], ints[:, HID:2 * HID]
        down_int = ints[:, 2 * HID:3 * HID].rearrange("p (c d) -> p c d", c=HT)
        bv_wide = stage[:, 4 * H * D + HV + 3 * HID:4 * H * D + 2 * HV + 3 * HID].rearrange("p (c n) -> p c n", c=NC)

        ps_s = pb("ps_s", [P, CH, 512])
        ps_t = [pb("ps_t0", [P, 512]), pb("ps_t1", [P, 512])]
        ps_o = pb("ps_o", [P, 512])
        ps_m = pb("ps_m", [P, 512])
        ps_h = [ps_o, ps_m]

        w_self = sem("w_self")
        w_cross = sem("w_cross")
        w_bias = sem("w_bias")
        bias_mul = sem("bias_mul")
        w_in = sem("w_in")
        x_got = sem("x_got")
        ctx_got = sem("ctx_got")
        out_put = sem("out_put")
        consts = sem("consts")
        fold_mm = sem("fold_mm")
        bias_done = sem("bias_done")
        fold_hi = sem("fold_hi")
        fold_cp = sem("fold_cp")
        prep = sem("prep")
        dve_step = sem("dve_step")
        wvhi_done = sem("wvhi_done")
        ctxhi_done = sem("ctxhi_done")
        ctxlo_done = sem("ctxlo_done")
        v_mm = sem("v_mm")
        v_cp = sem("v_cp")
        var_done = sem("var_done")
        rstd_done = sem("rstd_done")
        xn_done = [sem(f"xn_done{k}") for k in range(3)]
        xt_mm = [sem(f"xt_mm{k}") for k in range(3)]
        xt_cp = [sem(f"xt_cp{k}") for k in range(3)]
        xthi_done = [sem(f"xthi_done{k}") for k in range(2)]
        xtlo_done = [sem(f"xtlo_done{k}") for k in range(2)]
        qs_mm = sem("qs_mm")
        qs_cp = sem("qs_cp")
        logit_mm = sem("logit_mm")
        nmax_done = sem("nmax_done")
        es_done = sem("es_done")
        diag_done = sem("diag_done")
        vs_mm = sem("vs_mm")
        os_done = sem("os_done")
        ot_mm = sem("ot_mm")
        ot_cp = sem("ot_cp")
        ys_mm = sem("ys_mm")
        x1_done = sem("x1_done")
        t_mm = sem("t_mm")
        t_done = sem("t_done")
        q_mm = sem("q_mm")
        qhi_done = sem("qhi_done")
        qlo_done = sem("qlo_done")
        s_mm = sem("s_mm")
        ebias_done = sem("ebias_done")
        exp_done = sem("exp_done")
        pt_mm = sem("pt_mm")
        pt_act = sem("pt_act")
        pt_dve = sem("pt_dve")
        av_mm = sem("av_mm")
        rwide_done = sem("rwide_done")
        rt_mm = sem("rt_mm")
        rt_cp = sem("rt_cp")
        attn_done = sem("attn_done")
        y_mm = sem("y_mm")
        ffn_mm = sem("ffn_mm")
        sig_done = sem("sig_done")
        hact_done = sem("hact_done")
        down_mm = sem("down_mm")
        fin_done = sem("fin_done")

        block = ctx.enter_context(nc.Block())
        PRE_STEPS = 3
        FIRST_STEPS, SELF_STEPS, CROSS_STEPS, TAIL_STEPS = 2, 20, 129, 22
        NX = 3
        AV_CUT = (KT + 1) // 2
        V_HEAD = [0, 0] + [1] * (H - 2)
        V_OUT = (2, 1, 2, 3)
        V_ROWS, V_SCORES = 1, 1
        LAST_HIDDEN = 10
        assert sum(V_HEAD) + sum(V_OUT) + V_ROWS + V_SCORES + 2 == NV

        def batches(eng, self_part, cross_part, tail):
            self_part(0, False)
            with eng.Fori(1, B) as b:
                cross_part(b - 1, b)
                self_part(b, True)
            cross_part(B - 1, None)
            tail(B - 1)

        def v_bank(k):
            return ps_s[:, 2 + k % 2, :] if k < NV - 2 else (ps_o, ps_m)[k - (NV - 2)][:, :]

        def folded(weights, g):
            return weights[:, 8 * (g % 2):8 * (g % 2) + 8, :].rearrange("p (j a) d -> p a j d", a=2)

        def folded_bank(g):
            return ps_s[:, 2 * (g % 2):2 * (g % 2) + 2, :].rearrange("p a (j d) -> p a j d", d=D)

        @block.sync
        def _(sp):
            def load(s, dst, src):
                sp.dma_start(dst, src).then_inc(s, 16)

            def load_x(b):
                sp.dma_start(x_in[:, :, :], x[b].rearrange("(t p) d -> p t d", p=P)).then_inc(x_got, 16)

            def load_ctx(b):
                sp.dma_start(ctx_raw[:, 0:SK], ctx_t[b]).then_inc(ctx_got, 16)

            load_x(0)
            load(w_self, st_pq, pq_t)
            load(w_self, st_pk, pk_t)
            load(w_cross, st_wq, wq_t)
            load(w_cross, st_wk, wk_t)
            load(w_cross, w_wv, wv)
            load_ctx(0)
            rest = [
                (w_pv[:, :], pv), (w_po[:, :, :], po.rearrange("(c p) d -> p c d", p=P)),
                (w_wo[:, :, :], wo.rearrange("(c p) d -> p c d", p=P)),
                (bv_c[:, :], bv), (bo_in[:, :], bo.partition_broadcast(P)),
                (gamma_all[:, :], gamma.partition_broadcast(P)), (beta_all[:, :], beta.partition_broadcast(P)),
                (gate_int, w_gate_t), (up_int, w_up_t), (down_int, w_down_t.rearrange("(c p) d -> p c d", p=P)),
            ]
            assert len(rest) == N_REST
            for dst, src in rest:
                load(w_in, dst, src)
            for dst, src in ((wide_wq, wq), (wide_wk, wk), (wide_bq, bq.partition_broadcast(P)),
                             (wide_bk, bk.partition_broadcast(P))):
                load(w_bias, dst, src)
            with sp.Fori(1, B) as b:
                sp.wait_ge(x1_done, b)
                load_x(b)
                sp.wait_ge(ctxlo_done, b)
                load_ctx(b)

        @block.gpsimd
        def _(pool):
            pool.memset(ident[:, :], 0.0).then_inc(consts, 1)
            pool.memset(mask_b[:, :], 0.0).then_inc(consts, 1)
            pool.memset(nhalf[:, :], -0.5)
            pool.memset(ctx_raw[:, SK:SKP], 0.0)
            pool.wait_ge(consts, 2)
            pool.affine_select(out=ident[:, :], in_=ident[:, :], compare_op=ALU.not_equal, fill=1.0, base=0,
                               pattern=[[-1, P]], channel_multiplier=1).then_inc(consts, 1)
            pool.affine_select(out=mask_b[:, :], in_=mask_b[:, :], compare_op=ALU.is_ge, fill=MASKED, base=0,
                               pattern=[[-1, P]], channel_multiplier=1).then_inc(consts, 1)
            pool.wait_ge(consts, 4)
            pool.tensor_copy(ident_b[:, :], ident[:, :]).then_inc(consts, 1)
            pool.wait_ge(var_done, 1)
            pool.tensor_tensor(rstd[:, :], var[:, :], nhalf[:, :], ALU.pow).then_inc(rstd_done, 1)
            pool.wait_ge(w_bias, 64)
            pool.tensor_tensor(wide_wk, wide_wk, wide_bq, ALU.mult).then_inc(bias_mul, 1)
            pool.tensor_tensor(wide_wq, wide_wq, wide_bk, ALU.mult).then_inc(bias_mul, 1)
            pool.wait_ge(bias_mul, 2)
            pool.tensor_tensor(wide_bq, wide_bq, wide_bk, ALU.mult).then_inc(bias_mul, 1)
            with pool.Fori(1, 4 * B) as k:
                pool.wait_ge(var_done, k + 1)
                pool.tensor_tensor(rstd[:, :], var[:, :], nhalf[:, :], ALU.pow).then_inc(rstd_done, 1)

        @block.tensor
        def _(pe):
            pe.wait_ge(consts, 5)

            def transpose_rows(k, b):
                pe.wait_ge(xn_done[k], b + 1)
                for t in range(QT):
                    mm = pe.transpose(ps_m[:, t * P:(t + 1) * P], xn[k][:, t, :], ident[:, :])
                mm.then_inc(xt_mm[k], 1)

            transpose_rows(0, 0)
            for g in range(4):
                pe.wait_ge(w_self if g < 2 else w_cross, 32 if g < 2 else 48)
                wa, wb = (st_pq, st_pk) if g < 2 else (st_wq, st_wk)
                if g >= 2:
                    pe.wait_ge(fold_cp, g - 1)
                for j in range(4):
                    for a in range(2):
                        rows, p = slice(a * DK, (a + 1) * DK), 4 * (g % 2) + j
                        mm = pe.matmul(ps_s[:, 2 * (g % 2) + a, j * D:(j + 1) * D], wa[rows, p, :], wb[rows, p, :],
                                       start=True, stop=True)
                mm.then_inc(fold_mm, 1)

            def fold_bias():
                pe.wait_ge(prep, 2)
                pe.wait_ge(w_in, 16 * N_REST)
                for c in range(NC):
                    mm = pe.matmul(ps_o[:, 0:D], bv_wide[:, c, :], w_wo[:, c, :], start=(c == 0), stop=(c == NC - 1))
                mm.then_inc(fold_mm, 1)
                pe.wait_ge(fold_cp, 4)
                pe.wait_ge(wvhi_done, 1)

            def project_out(b):
                pe.wait_ge(attn_done, b * NJ + NJ)
                for t in range(QT):
                    for c in range(NP):
                        mm = pe.matmul(ps_o[:, t * P:(t + 1) * P], attn_t[:, c, t * P:(t + 1) * P], w_wo[:, c, :],
                                       start=(c == 0), stop=(c == NP - 1))
                mm.then_inc(y_mm, 1)

            def gate_up(b, c):
                bank = ps_h[c % 2]
                if c == 0:
                    pe.wait_ge(xt_cp[2], b + 1)
                if c >= 2:
                    pe.wait_ge(hact_done, b * HT + (c - 1))
                pe.matmul(bank[:, 0:SQ], gate_w[:, c * P:(c + 1) * P], xt[2][:, :], start=True, stop=True)
                pe.matmul(bank[:, SQ:2 * SQ], up_w[:, c * P:(c + 1) * P], xt[2][:, :], start=True,
                          stop=True).then_inc(ffn_mm, 1)

            def down(b):
                pe.wait_ge(hact_done, b * HT + HT)
                for t in range(QT):
                    for c in range(HT):
                        mm = pe.matmul(ps_o[:, t * P:(t + 1) * P], h_act[:, c, t * P:(t + 1) * P], down_w[:, c, :],
                                       start=(c == 0), stop=(c == HT - 1))
                mm.then_inc(down_mm, 1)

            def tail(b):
                project_out(b)
                transpose_rows(2, b)
                for c in range(HT):
                    gate_up(b, c)
                down(b)

            def values(b, first, n):
                for k in range(first, first + n):
                    i, half = k // 2, k % 2
                    rows = P if i < KT - 1 else KL
                    keys, cols = slice(i * P, i * P + rows), slice(half * 512, half * 512 + 512)
                    if k == 0:
                        pe.wait_ge(ctxhi_done, b + 1)
                        pe.wait_ge(ctxlo_done, b + 1)
                    if k >= 2:
                        pe.wait_ge(v_cp, b * NV + (k - 1))
                    if k == NV - 2:
                        pe.wait_ge(t_done, b + 1)
                    if k == NV - 1:
                        pe.wait_ge(qlo_done, b * NP + 1)
                    dst = v_bank(k)[0:rows, :]
                    pe.matmul(dst, ctx_hi[:, keys], wv_hi[:, cols], start=True, stop=False)
                    pe.matmul(dst, ctx_hi[:, keys], wv_lo[:, cols], start=False, stop=False)
                    pe.matmul(dst, ctx_lo[:, keys], wv_hi[:, cols], start=False, stop=True).then_inc(v_mm, 1)

            def split_product(dst, w_hi, w_lo, k):
                pe.matmul(dst, w_hi, xt_hi[k][:, :], start=True, stop=False)
                pe.matmul(dst, w_lo, xt_hi[k][:, :], start=False, stop=False)
                return pe.matmul(dst, w_hi, xt_lo[k][:, :], start=False, stop=True)

            def self_q(b, p, follows):
                if p >= 2:
                    pe.wait_ge(qs_cp, b * NP + (p - 1))
                elif follows:
                    pe.wait_ge(pt_act if p == 0 else pt_dve, b * NU * 2)
                for a in range(2):
                    mm = split_product(ps_t[p % 2][:, a * SQ:(a + 1) * SQ], qk_self_hi[:, 2 * p + a, :],
                                       qk_self_lo[:, 2 * p + a, :], 0)
                mm.then_inc(qs_mm, 1)

            def self_part(b, follows):
                if not follows:
                    pe.wait_ge(fold_cp, 2)
                    pe.wait_ge(xt_cp[0], b + 1)
                    pe.wait_ge(xthi_done[0], b + 1)
                    pe.wait_ge(xtlo_done[0], b + 1)
                    self_q(b, 0, follows)
                    fold_bias()
                for h in range(H):
                    if h % 2 == 0 and h // 2 + 1 < NP:
                        self_q(b, h // 2 + 1, follows)
                    values(b, sum(V_HEAD[:h]), V_HEAD[h])
                    pe.wait_ge(qs_cp, b * NP + (h // 2 + 1))
                    if h >= 2:
                        pe.wait_ge(es_done, b * H + (h - 1))
                    q = qs[:, (h // 2) % 2, (h % 2) * SQ:(h % 2 + 1) * SQ]
                    bank = ps_s[:, h % 2, :]
                    pe.matmul(bank[:, 0:P], q[:, 0:P], xt[0][:, 0:P], start=True, stop=False)
                    pe.matmul(bank[:, 0:P], ident_b[:, :], mask_b[:, :], start=False, stop=True)
                    pe.matmul(bank[:, P:P + SQ], q[:, P:SQ], xt[0][:, :], start=True, stop=False)
                    pe.matmul(bank[:, 2 * P:3 * P], ident_b[:, :], mask_b[:, :], start=False,
                              stop=True).then_inc(logit_mm, 1)
                    if follows and h == 1:
                        project_out(b - 1)
                    if follows and h == 5:
                        transpose_rows(2, b - 1)
                    if follows and h == 6:
                        gate_up(b - 1, 0)
                        gate_up(b - 1, 1)
                    if follows and h == LAST_HIDDEN:
                        gate_up(b - 1, 2)

                def self_values(t):
                    if t == 0:
                        pe.wait_ge(qs_cp, b * NP + NP)
                    else:
                        pe.wait_ge(os_done, b * QT + t)
                    for n in range(2):
                        mm = pe.matmul(ps_t[n][:, :], xt[0][:, t * P:(t + 1) * P], w_pv[:, n * 512:(n + 1) * 512],
                                       start=True, stop=True)
                    mm.then_inc(vs_mm, 1)

                def turn_self(t):
                    pe.wait_ge(os_done, b * QT + (t + 1))
                    if t == 0:
                        pe.wait_ge(es_done, b * H + H)
                    for c in range(NC):
                        mm = pe.transpose(ps_s[:, c // 4, (c % 4) * P:(c % 4 + 1) * P],
                                          o_self[:, t, c * P:(c + 1) * P], ident[:, :])
                    mm.then_inc(ot_mm, 1)

                def project_self(t):
                    pe.wait_ge(ot_cp, b * QT + (t + 1))
                    if t == 0:
                        if follows:
                            pe.wait_ge(fin_done, b)
                        else:
                            pe.wait_ge(fold_cp, 5)
                    for c in range(NC):
                        mm = pe.matmul(ps_o[:, t * P:(t + 1) * P], o_self_t[:, c, :], w_po[:, c, :],
                                       start=(c == 0), stop=(c == NC - 1))
                    mm.then_inc(ys_mm, 1)

                self_values(0)
                values(b, sum(V_HEAD) + sum(V_OUT[:0]), V_OUT[0])
                if follows:
                    down(b - 1)
                turn_self(0)
                self_values(1)
                values(b, sum(V_HEAD) + sum(V_OUT[:1]), V_OUT[1])
                project_self(0)
                turn_self(1)
                values(b, sum(V_HEAD) + sum(V_OUT[:2]), V_OUT[2])
                project_self(1)
                values(b, sum(V_HEAD) + sum(V_OUT[:3]), V_OUT[3])

            def cross_part(b, nxt):
                transpose_rows(1, b)
                values(b, NV - 2 - V_SCORES - V_ROWS, V_ROWS)
                pe.wait_ge(xt_cp[1], b + 1)
                pe.wait_ge(bias_done, 1)
                for t in range(QT):
                    mm = pe.matmul(ps_o[:, t * H:(t + 1) * H], xt[1][:, t * P:(t + 1) * P], ub[:, :],
                                   start=True, stop=True)
                mm.then_inc(t_mm, 1)

                def cross_q(p):
                    for a in range(2):
                        mm = split_product(ps_m[:, a * SQ:(a + 1) * SQ], qk_cross_hi[:, 2 * p + a, :],
                                           qk_cross_lo[:, 2 * p + a, :], 1)
                    mm.then_inc(q_mm, 1)

                def scores(u):
                    p, t, a = u // 4, u // 2 % 2, u % 2
                    at = a * SQ + t * P
                    hi, lo = q_hi[:, p % 2, at:at + P], q_lo[:, p % 2, at:at + P]
                    pe.wait_ge(qhi_done, b * NP + (p + 1))
                    pe.wait_ge(qlo_done, b * NP + (p + 1))
                    if u == 0:
                        pe.wait_ge(v_cp, b * NV + NV - 2)
                    for c in range(CH):
                        if u > 0 and c != 1:
                            pe.wait_ge(exp_done, b * NU * NX + (NX * (u - 1) + max(c, 1)))
                        n = CW if c < CH - 1 else SKP - (CH - 1) * CW
                        keys, dst = slice(c * CW, c * CW + n), ps_s[:, c, 0:n]
                        pe.matmul(dst, hi, ctx_hi[:, keys], start=True, stop=False)
                        pe.matmul(dst, hi, ctx_lo[:, keys], start=False, stop=False)
                        pe.matmul(dst, lo, ctx_hi[:, keys], start=False, stop=True).then_inc(s_mm, 1)

                def transposes(u, groups):
                    for g in groups:
                        if g < NX:
                            pe.wait_ge(exp_done, b * NU * NX + (NX * u + g + 1))
                        if u > 0 or g >= 2:
                            pe.wait_ge(pt_act if g % 2 == 0 else pt_dve, b * NU * 2 + (2 * u + g // 2))
                        for i in range(4 * g, min(4 * g + 4, KT)):
                            n = P if i < KT - 1 else KL
                            mm = pe.transpose(ps_t[g % 2][0:n, (i % 4) * P:(i % 4 + 1) * P],
                                              probs[:, u % 2, i * P:i * P + n], ident[:, :])
                        mm.then_inc(pt_mm, 1)

                def weigh(j, part):
                    p = j // QT
                    if part == 0:
                        pe.wait_ge(pt_act, b * NU * 2 + (4 * j + 3))
                        pe.wait_ge(pt_dve, b * NU * 2 + (4 * j + 3))
                        if j == 0:
                            pe.wait_ge(t_done, b + 1)
                        else:
                            pe.wait_ge(attn_done, b * NJ + j)
                    else:
                        pe.wait_ge(pt_act, b * NU * 2 + 4 * (j + 1))
                        pe.wait_ge(pt_dve, b * NU * 2 + 4 * (j + 1))
                    for i in range(0, AV_CUT) if part == 0 else range(AV_CUT, KT):
                        rows = P if i < KT - 1 else KL
                        for a in range(2):
                            at = (2 * p + a) * DK
                            mm = pe.matmul(ps_o[a * DK:(a + 1) * DK, 0:P], vals[0:rows, i, at:at + DK],
                                           probs_t[0:rows, j % 2, a, i, :], start=(i == 0), stop=(i == KT - 1),
                                           skip_group_check=True)
                    if part == 1:
                        mm.then_inc(av_mm, 1)

                def turn_weights(j):
                    pe.wait_ge(rwide_done, b * NJ + (j + 1))
                    if j > 0:
                        pe.wait_ge(rt_cp, b * NJ + j)
                    pe.wait_ge(qlo_done, b * NP + min((2 * j + 4) // 4 + 1, NP))
                    pe.transpose(ps_m[:, 0:P], rwide[:, :, :].rearrange("p a k -> p (a k)"),
                                 ident[:, :]).then_inc(rt_mm, 1)

                pe.wait_ge(xthi_done[1], b + 1)
                pe.wait_ge(xtlo_done[1], b + 1)
                cross_q(0)
                values(b, NV - 2 - V_SCORES, V_SCORES)
                scores(0)
                values(b, NV - 2, 2)
                for u in range(NU):
                    if u + 1 < NU:
                        scores(u + 1)
                    if u == 0:
                        pe.wait_ge(v_cp, b * NV + NV)
                    if u == NU - 1:
                        weigh(u // 2 - 1, u % 2)
                    transposes(u, (0, 1))
                    if 2 <= u < NU - 1:
                        weigh(u // 2 - 1, u % 2)
                    transposes(u, range(2, TG))
                    if u >= 2:
                        if u % 2 == 0:
                            turn_weights(u // 2 - 1)
                    if u % 4 == 1 and u // 4 + 1 < NP:
                        if u > 4:
                            pe.wait_ge(rt_cp, b * NJ + (u // 2))
                        cross_q(u // 4 + 1)
                if nxt is not None:
                    pe.wait_ge(rt_cp, b * NJ + (NJ - 1))
                    transpose_rows(0, nxt)
                weigh(NJ - 1, 0)
                if nxt is not None:
                    pe.wait_ge(xt_cp[0], nxt + 1)
                    pe.wait_ge(xthi_done[0], nxt + 1)
                    pe.wait_ge(xtlo_done[0], nxt + 1)
                    self_q(nxt, 0, True)
                turn_weights(NJ - 1)
                weigh(NJ - 1, 1)

            batches(pe, self_part, cross_part, tail)

        @block.scalar
        def _(act):
            def copy_rows(k, b):
                act.wait_ge(xt_mm[k], b + 1)
                if k < 2:
                    act.activation(xt_hi[k][:, :], ps_m[:, 0:SQ], ACT.Copy).then_inc(xthi_done[k], 1)
                act.activation(xt[k][:, :], ps_m[:, 0:SQ], ACT.Copy).then_inc(xt_cp[k], 1)

            copy_rows(0, 0)
            for g in range(4):
                if g == 2:
                    act.wait_ge(w_cross, 48)
                    act.activation(wv_hi[:, :], w_wv, ACT.Copy).then_inc(wvhi_done, 1)
                act.wait_ge(fold_mm, g + 1)
                act.activation(folded((qk_self_hi, qk_cross_hi)[g // 2], g), folded_bank(g),
                               ACT.Copy).then_inc(fold_hi, 1)

            def gate_exp(b, c):
                act.wait_ge(ffn_mm, b * HT + (c + 1))
                act.activation(h_e[:, c, :], ps_h[c % 2][:, 0:SQ], ACT.Exp, scale=-1.0).then_inc(sig_done, 1)

            def store(b):
                act.wait_ge(fin_done, b + 1)
                act.dma_start(out[b].rearrange("(t p) d -> p t d", p=P), fin[:, :, :]).then_inc(out_put, 16)

            def tail(b):
                copy_rows(2, b)
                for c in range(HT):
                    gate_exp(b, c)
                store(b)
                act.wait_ge(out_put, 16 * (b + 1))

            def values(b, first, n):
                for k in range(first, first + n):
                    rows = P if k // 2 < KT - 1 else KL
                    act.wait_ge(v_mm, b * NV + (k + 1))
                    act.activation(vals[0:rows, k // 2, (k % 2) * 512:(k % 2 + 1) * 512],
                                   v_bank(k)[0:rows, :], ACT.Copy).then_inc(v_cp, 1)

            def self_q(b, p):
                act.wait_ge(qs_mm, b * NP + (p + 1))
                if p >= 2:
                    act.wait_ge(logit_mm, b * H + 2 * (p - 1))
                act.activation(qs[:, p % 2, :], ps_t[p % 2][:, :], ACT.Copy).then_inc(qs_cp, 1)

            def split_ctx(b, follows):
                act.wait_ge(ctx_got, b * 16 + 16)
                if follows:
                    act.wait_ge(s_mm, b * NU * CH)
                act.activation(ctx_hi[:, :], ctx_raw[:, :], ACT.Copy).then_inc(ctxhi_done, 1)

            def self_part(b, follows):
                if not follows:
                    act.wait_ge(consts, 5)
                    split_ctx(b, follows)
                    self_q(b, 0)
                for h in range(H):
                    if h % 2 == 0 and h // 2 + 1 < NP:
                        self_q(b, h // 2 + 1)
                    values(b, sum(V_HEAD[:h]), V_HEAD[h])
                    act.wait_ge(nmax_done, b * H + (h + 1))
                    if h >= 2:
                        act.wait_ge(diag_done, b * H + (h - 1))
                    for t in range(QT):
                        lo, n = t * P, (t + 1) * P
                        ins = act.activation(es[:, h % 2, lo:lo + n], ps_s[:, h % 2, lo:lo + n], ACT.Exp,
                                             bias=nmx8[:, h, t:t + 1], scale=SHARP, accum_out=sums_s[:, t, h:h + 1])
                    ins.then_inc(es_done, 1)
                    if follows and h == 5:
                        copy_rows(2, b - 1)
                    if follows and h == 6:
                        gate_exp(b - 1, 0)
                        gate_exp(b - 1, 1)
                    if follows and h == LAST_HIDDEN:
                        gate_exp(b - 1, 2)

                def copy_self(t):
                    act.wait_ge(ot_mm, b * QT + (t + 1))
                    if t > 0:
                        act.wait_ge(ys_mm, b * QT + t)
                    act.activation(o_self_t[:, :, :], ps_s[:, 0:2, :].rearrange("p b (c n) -> p (b c) n", n=P),
                                   ACT.Copy).then_inc(ot_cp, 1)

                values(b, sum(V_HEAD) + sum(V_OUT[:0]), V_OUT[0])
                copy_self(0)
                values(b, sum(V_HEAD) + sum(V_OUT[:1]), V_OUT[1])
                copy_self(1)
                values(b, sum(V_HEAD) + sum(V_OUT[:2]), V_OUT[2])
                if follows:
                    store(b - 1)
                values(b, sum(V_HEAD) + sum(V_OUT[:3]), V_OUT[3])
                if follows:
                    act.wait_ge(out_put, b * 16)

            def cross_part(b, nxt):
                copy_rows(1, b)
                values(b, NV - 2 - V_SCORES - V_ROWS, V_ROWS)

                def cross_q_hi(p):
                    act.wait_ge(q_mm, b * NP + (p + 1))
                    for a in range(2):
                        ins = act.activation(q_hi[:, p % 2, a * SQ:(a + 1) * SQ], ps_m[:, a * SQ:(a + 1) * SQ],
                                             ACT.Identity, bias=qbias[:, 2 * p + a:2 * p + a + 1])
                    ins.then_inc(qhi_done, 1)

                def exps(u):
                    act.wait_ge(ebias_done, b * NU + (u + 1))
                    if u >= 2:
                        act.wait_ge(pt_mm, b * NU * TG + TG * (u - 1))
                    for k in range(NX):
                        c, n = (0, 2) if k == 0 else (k + 1, 1)
                        w = CW if c < CH - 1 else CL
                        act.activation(probs[:, u % 2, c * CW:c * CW + n * w].rearrange("p (c k) -> p c k", c=n),
                                       ps_s[:, c:c + n, 0:w], ACT.Exp, bias=ebias[:, u % 2:u % 2 + 1], scale=TEMP,
                                       accum_out=sums[:, u % 8, k:k + 1]).then_inc(exp_done, 1)

                def copy_group(u, g):
                    j, a = u // 2, u % 2
                    act.wait_ge(pt_mm, b * NU * TG + (TG * u + g + 1))
                    if g == 0 and j >= 2:
                        act.wait_ge(av_mm, b * NJ + (j - 1))
                    n = min(4, KT - 4 * g)
                    act.activation(probs_t[:, j % 2, a, 4 * g:4 * g + n, :],
                                   ps_t[0][:, 0:n * P].rearrange("p (i q) -> p i q", q=P),
                                   ACT.Copy).then_inc(pt_act, 1)

                def copy_weights(j):
                    act.wait_ge(rt_mm, b * NJ + (j + 1))
                    if j > 0:
                        act.wait_ge(attn_done, b * NJ + j)
                    act.activation(rt[:, :], ps_m[:, 0:P], ACT.Copy).then_inc(rt_cp, 1)

                cross_q_hi(0)
                values(b, NV - 2 - V_SCORES, V_SCORES)
                values(b, NV - 2, 2)
                exps(0)
                for u in range(NU):
                    copy_group(u, 0)
                    if u % 4 == 2 and u // 4 + 1 < NP:
                        cross_q_hi(u // 4 + 1)
                    if u + 1 < NU:
                        exps(u + 1)
                    copy_group(u, 2)
                    if u % 2 == 0 and u > 0:
                        copy_weights(u // 2 - 1)
                if nxt is not None:
                    copy_rows(0, nxt)
                    split_ctx(nxt, True)
                    self_q(nxt, 0)
                copy_weights(NJ - 1)

            batches(act, self_part, cross_part, tail)

        @block.vector
        def _(dve):
            steps, base = [0], [0]

            def then(ins):
                steps[0] += 1
                ins.then_inc(dve_step, 1)
                dve.wait_ge(dve_step, base[0] + steps[0])

            def moments(src):
                for t in range(QT):
                    ins = dve.bn_stats(stats[:, t, :], src[:, t, :])
                then(ins)
                dve.memset(spare[:, :], 0.0)
                for t in range(QT):
                    ins = dve.bn_aggr(mv[:, t, :], stats[:, t, :])
                then(ins)
                dve.tensor_scalar(var[:, :], mv[:, :, 1], EPS, None, ALU.add).then_inc(var_done, 1)

            def scaled(k, src, dst):
                dve.wait_ge(rstd_done, k + 1)
                for t in range(QT):
                    ins = dve.tensor_scalar(dst[:, t, :], src[:, t, :], mv[:, t, 0:1], rstd[:, t:t + 1],
                                            ALU.subtract, ALU.mult)
                return ins

            def normalise(k, src, dst):
                moments(src)
                return scaled(k, src, dst)

            def rows_rest(k, b):
                dve.wait_ge(xt_cp[k], b + 1)
                dve.wait_ge(xthi_done[k], b + 1)
                dve.tensor_tensor(xt_lo[k][:, :], xt[k][:, :], xt_hi[k][:, :].bitcast(F32),
                                  ALU.subtract).then_inc(xtlo_done[k], 1)

            dve.wait_ge(x_got, 16)
            normalise(0, x_in, xn[0]).then_inc(xn_done[0], 1)
            rows_rest(0, 0)
            for g in range(4):
                if g == 2:
                    dve.wait_ge(wvhi_done, 1)
                    dve.tensor_tensor(wv_lo[:, :], w_wv, wv_hi[:, :].bitcast(F32), ALU.subtract).then_inc(prep, 1)
                hi, lo = ((qk_self_hi, qk_self_lo), (qk_cross_hi, qk_cross_lo))[g // 2]
                dve.wait_ge(fold_hi, g + 1)
                dve.tensor_tensor(folded(lo, g), folded_bank(g), folded(hi, g).bitcast(F32),
                                  ALU.subtract).then_inc(fold_cp, 1)
            dve.wait_ge(w_in, 16 * N_REST)
            dve.tensor_copy(bv_wide, bv_c[:, :].unsqueeze(2).broadcast_to([P, NC, P])).then_inc(prep, 1)
            dve.tensor_scalar(gate_w[:, :], gate_int, 1.0 / 127.0, None, ALU.mult)
            dve.tensor_scalar(up_w[:, :], up_int, 1.0 / 127.0, None, ALU.mult)
            then(dve.tensor_scalar(down_w[:, :, :], down_int, 1.0 / 127.0, None, ALU.mult))
            dve.wait_ge(fold_mm, 5)
            dve.tensor_tensor(bo_all[:, :], ps_o[:, 0:D], bo_in[:, :], ALU.add).then_inc(fold_cp, 1)
            assert steps[0] == PRE_STEPS
            steps[0], base[0] = 0, PRE_STEPS

            def both(row):
                return row[:, :].unsqueeze(1).broadcast_to([P, QT, D])

            def tail_rows(b, k, parts=(0, 1, 2)):
                if 0 in parts:
                    dve.wait_ge(y_mm, b + 1)
                    then(dve.tensor_tensor(y[:, :, :], ps_o[:, 0:SQ].rearrange("p (t d) -> p t d", d=D), both(bo_all),
                                           ALU.add))
                    then(dve.tensor_tensor(y[:, :, :], y[:, :, :], xn[1][:, :, :], ALU.add))
                    moments(y)
                if 1 in parts:
                    then(scaled(k, y, y))
                    then(dve.tensor_tensor(y[:, :, :], y[:, :, :], both(gamma_all), ALU.mult))
                    then(dve.tensor_tensor(y[:, :, :], y[:, :, :], both(beta_all), ALU.add))
                    then(dve.tensor_tensor(x2[:, :, :], x1[:, :, :], y[:, :, :], ALU.add))
                    moments(x2)
                if 2 in parts:
                    scaled(k + 1, x2, xn[2]).then_inc(xn_done[2], 1)

            def tail_hidden(b, c, parts=(0, 1, 2)):
                if 0 in parts:
                    dve.wait_ge(sig_done, b * HT + (c + 1))
                    then(dve.tensor_scalar(h_e[:, c, :], h_e[:, c, :], 1.0, None, ALU.add))
                    then(dve.reciprocal(h_e[:, c, 0:P], h_e[:, c, 0:P]))
                if 1 in parts:
                    then(dve.reciprocal(h_e[:, c, P:SQ], h_e[:, c, P:SQ]))
                if 2 in parts:
                    bank = ps_h[c % 2]
                    then(dve.tensor_tensor(h_e[:, c, :], bank[:, 0:SQ], h_e[:, c, :], ALU.mult))
                    dve.tensor_tensor(h_act[:, c, :], bank[:, SQ:2 * SQ], h_e[:, c, :],
                                      ALU.mult).then_inc(hact_done, 1)

            def tail_out(b):
                dve.wait_ge(down_mm, b + 1)
                dve.tensor_tensor(fin[:, :, :], ps_o[:, 0:SQ].rearrange("p (t d) -> p t d", d=D), x2[:, :, :],
                                  ALU.add).then_inc(fin_done, 1)

            def tail(b):
                tail_rows(b, 4 * b + 2)
                for c in range(HT):
                    tail_hidden(b, c)
                dve.wait_ge(out_put, b * 16)
                tail_out(b)

            def ctx_rest(b):
                dve.wait_ge(ctxhi_done, b + 1)
                dve.tensor_tensor(ctx_lo[:, :], ctx_raw[:, :], ctx_hi[:, :].bitcast(F32),
                                  ALU.subtract).then_inc(ctxlo_done, 1)

            def self_part(b, follows):
                if not follows:
                    ctx_rest(b)

                def diagonal(h):
                    dve.wait_ge(es_done, b * H + (h + 1))
                    for t in range(QT):
                        ins = dve.scalar_tensor_tensor(out=junk[:, h % 2, t, :],
                                                       in0=es[:, h % 2, 2 * t * P:(2 * t + 1) * P],
                                                       scalar=1.0, in1=ident[:, :], op0=ALU.mult, op1=ALU.mult,
                                                       accum_out=diag_s[:, t, h:h + 1])
                    ins.then_inc(diag_done, 1)

                for h in range(H):
                    if follows and 2 <= h < 5:
                        tail_rows(b - 1, 4 * b - 1, (h - 2,))
                    dve.wait_ge(logit_mm, b * H + (h + 1))
                    for t in range(QT):
                        lo, n = t * P, (t + 1) * P
                        ins = dve.tensor_reduce(nmx[:, h, t:t + 1], ps_s[:, h % 2, lo:lo + n], AX.X, ALU.max,
                                                negate=True)
                    then(ins)
                    dve.tensor_scalar(nmx8[:, h, :], nmx[:, h, :], SHARP, None, ALU.mult).then_inc(nmax_done, 1)
                    if h > 0:
                        diagonal(h - 1)
                    if follows and 6 <= h < 6 + 3 * HT:
                        tail_hidden(b - 1, (h - 6) // 3, ((h - 6) % 3,))
                diagonal(H - 1)
                then(dve.reciprocal(rsum_s[:, :, :], sums_s[:, :, :]))
                dve.wait_ge(diag_done, b * H + H)
                then(dve.tensor_tensor(wdiag[:, :, :], diag_s[:, :, :], rsum_s[:, :, :], ALU.mult))
                for t in range(QT):
                    dve.wait_ge(vs_mm, b * QT + (t + 1))
                    for n in range(2):
                        w = wdiag[:, t, 8 * n:8 * n + 8].unsqueeze(2).broadcast_to([P, 8, DK])
                        ins = dve.tensor_tensor(o_self[:, t, n * 512:(n + 1) * 512].rearrange("p (h k) -> p h k", k=DK),
                                                ps_t[n][:, :].rearrange("p (h k) -> p h k", k=DK), w, ALU.mult)
                    ins.then_inc(os_done, 1)
                    if follows and t == 0:
                        tail_out(b - 1)
                    if not follows and t == 0:
                        for k, (dst, src) in enumerate(((qbias, wide_wk), (ub, wide_wq), (t0, wide_bq))):
                            dve.wait_ge(bias_mul, k + 1)
                            ins = dve.tensor_reduce(dst[:, :], src.rearrange("p (h k) -> p h k", k=DK), AX.X, ALU.add)
                        ins.then_inc(bias_done, 1)
                dve.wait_ge(ys_mm, b * QT + QT)
                ins = dve.tensor_tensor(x1[:, :, :], ps_o[:, 0:SQ].rearrange("p (t d) -> p t d", d=D), x_in[:, :, :],
                                        ALU.add)
                ins.then_inc(x1_done, 1)
                dve.wait_ge(x1_done, b + 1)
                normalise(4 * b + 1, x1, xn[1]).then_inc(xn_done[1], 1)

                assert steps[0] == (SELF_STEPS if not follows else CROSS_STEPS + FIRST_STEPS + TAIL_STEPS + SELF_STEPS)

            def cross_part(b, nxt):
                steps[0] = 0
                base[0] = b * (CROSS_STEPS + FIRST_STEPS + TAIL_STEPS + SELF_STEPS) + (PRE_STEPS + SELF_STEPS)
                rows_rest(1, b)
                dve.wait_ge(t_mm, b + 1)
                for t in range(QT):
                    ins = dve.tensor_tensor(tterm[:, t, :], ps_o[:, t * H:(t + 1) * H], t0[:, :], ALU.add)
                then(ins)
                dve.tensor_scalar(tterm8[:, :, :], tterm[:, :, :], TEMP, None, ALU.mult).then_inc(t_done, 1)
                dve.wait_ge(t_done, b + 1)

                def cross_q_lo(p):
                    dve.wait_ge(qhi_done, b * NP + (p + 1))
                    for a in range(2):
                        cols = slice(a * SQ, (a + 1) * SQ)
                        ins = dve.scalar_tensor_tensor(out=q_lo[:, p % 2, cols], in0=ps_m[:, cols],
                                                       scalar=qbias[:, 2 * p + a:2 * p + a + 1],
                                                       in1=q_hi[:, p % 2, cols].bitcast(F32),
                                                       op0=ALU.add, op1=ALU.subtract)
                    ins.then_inc(qlo_done, 1)

                def maxima(u):
                    h, t = 2 * (u // 4) + u % 2, u // 2 % 2
                    for c in range(CH):
                        dve.wait_ge(s_mm, b * NU * CH + (CH * u + c + 1))
                        ins = dve.tensor_reduce(mx4[:, c:c + 1], ps_s[:, c, 0:CW if c < CH - 1 else CL], AX.X, ALU.max)
                        if c == CH - 2:
                            then(ins)
                            ins = dve.tensor_reduce(mx3[:, :], mx4[:, 0:CH - 1], AX.X, ALU.max)
                    then(ins)
                    then(dve.scalar_tensor_tensor(out=nb[:, :], in0=mx4[:, CH - 1:CH], scalar=mx3[:, :],
                                                  in1=tterm[:, t, h:h + 1], op0=ALU.max, op1=ALU.add))
                    if u >= 2:
                        dve.wait_ge(exp_done, b * NU * NX + NX * (u - 1))
                    dve.scalar_tensor_tensor(out=ebias[:, u % 2:u % 2 + 1], in0=nb[:, :], scalar=-TEMP,
                                             in1=tterm8[:, t, h:h + 1], op0=ALU.mult,
                                             op1=ALU.add).then_inc(ebias_done, 1)

                def copy_group(u, g):
                    j, a = u // 2, u % 2
                    dve.wait_ge(pt_mm, b * NU * TG + (TG * u + g + 1))
                    if g == 1 and j >= 2:
                        dve.wait_ge(av_mm, b * NJ + (j - 1))
                    n = min(4, KT - 4 * g)
                    rows = P if g < TG - 1 else KL
                    dve.tensor_copy(probs_t[0:rows, j % 2, a, 4 * g:4 * g + n, :],
                                    ps_t[1][0:rows, 0:n * P].rearrange("p (i q) -> p i q", q=P)).then_inc(pt_dve, 1)

                def weights_wide(j):
                    s0 = 2 * (j % 4)
                    dve.wait_ge(exp_done, b * NU * NX + NX * (2 * j + 2))
                    then(dve.tensor_reduce(sum1[:, :], sums[:, s0:s0 + 2, :], AX.X, ALU.add))
                    then(dve.reciprocal(rsum[:, :], sum1[:, :]))
                    if j > 0:
                        dve.wait_ge(rt_mm, b * NJ + j)
                    dve.tensor_copy(rwide[:, :, :],
                                    rsum[:, :].unsqueeze(2).broadcast_to([P, 2, DK])).then_inc(rwide_done, 1)

                def normal_out(j):
                    p, t = j // QT, j % QT
                    dve.wait_ge(rt_cp, b * NJ + (j + 1))
                    dve.wait_ge(av_mm, b * NJ + (j + 1))
                    dve.tensor_tensor(attn_t[:, p, t * P:(t + 1) * P], ps_o[:, 0:P], rt[:, :],
                                      ALU.mult).then_inc(attn_done, 1)

                cross_q_lo(0)
                maxima(0)
                for u in range(NU):
                    if u % 2 == 0 and u >= 4:
                        normal_out(u // 2 - 2)
                    if u + 1 < NU:
                        maxima(u + 1)
                    copy_group(u, 1)
                    if u % 4 == 2 and u // 4 + 1 < NP:
                        cross_q_lo(u // 4 + 1)
                    if u == NU - 1:
                        normal_out(NJ - 2)
                    copy_group(u, 3)
                    if u % 2 == 1:
                        weights_wide(u // 2)
                    if nxt is not None and u == NU - 4:
                        dve.wait_ge(x_got, nxt * 16 + 16)
                        moments(x_in)
                    if nxt is not None and u == NU - 3:
                        scaled(4 * nxt - 2, x_in, xn[0]).then_inc(xn_done[0], 1)
                if nxt is not None:
                    rows_rest(0, nxt)
                    ctx_rest(nxt)
                normal_out(NJ - 1)
                assert steps[0] == CROSS_STEPS + (FIRST_STEPS if nxt is not None else 0)

            batches(dve, self_part, cross_part, tail)


def kernel(**inputs):
    import numpy as np
    import concourse.bacc as bacc
    from concourse.bass_utils import run_bass_kernel_spmd

    a = {k: np.asarray(v) for k, v in inputs.items()}

    def pairs(w):
        h, k, d = w.shape
        return w.reshape(h // 2, 2, k, d).transpose(1, 2, 0, 3).reshape(2 * k, h // 2, d)

    def by_head(w):
        return w.reshape(w.shape[0], -1, 64).transpose(1, 2, 0)

    laid = {
        "x": a["x"],
        "ctx_t": a["ctx_1024"].transpose(0, 2, 1),
        "pq_t": pairs(a["L0_attn_P_q"].transpose(0, 2, 1)),
        "pk_t": pairs(a["L0_attn_P_k"].transpose(0, 2, 1)),
        "pv": a["L0_attn_P_v"].transpose(1, 0, 2).reshape(128, -1),
        "po": a["L0_attn_P_o"].transpose(0, 2, 1).reshape(-1, 128),
        "wq_t": pairs(by_head(a["L0_xattn_Wq"])),
        "wk_t": pairs(by_head(a["L0_xattn_Wk"])),
        "wq": a["L0_xattn_Wq"],
        "wk": a["L0_xattn_Wk"],
        "bq": a["L0_xattn_bq"],
        "bk": a["L0_xattn_bk"],
        "wv": a["L0_xattn_Wv"],
        "bv": a["L0_xattn_bv"].reshape(-1, 128).T,
        "wo": a["L0_xattn_Wo"],
        "bo": a["L0_xattn_bo"],
        "gamma": a["L0_xattn_ln_gamma"],
        "beta": a["L0_xattn_ln_beta"],
        "w_gate_t": a["L0_ffn_w_gate"].T,
        "w_up_t": a["L0_ffn_w_up"].T,
        "w_down_t": a["L0_ffn_w_down"].T,
    }
    nc = bacc.Bacc("TRN2", target_bir_lowering=False, num_devices=1)
    arrays, args = {}, []
    for name, v in laid.items():
        v = np.ascontiguousarray(v)
        arrays[f"in_{name}"] = v
        args.append(nc.dram_tensor(f"in_{name}", v.shape, mybir.dt.from_np(v.dtype), kind="ExternalInput").ap())
    out = nc.dram_tensor("out_x", a["x"].shape, F32, kind="ExternalOutput").ap()
    decoder_layer(nc, *args, out)
    r = run_bass_kernel_spmd(nc, [arrays], core_ids=[0])
    return r.results[0]["out_x"]
```
